# Optimizing a Trainium2 kernel written in Bass

```python
import numpy as np
import jax
import jax.numpy as jnp

def _softmax(x, axis=-1):
    return jax.nn.softmax(x, axis=axis)

def _gelu(x):
    return jax.nn.gelu(x, approximate=True)

def _silu(x):
    return jax.nn.silu(x)

def _sigmoid(x):
    return jax.nn.sigmoid(x)

def _layernorm(x, axis=-1, eps=1e-05):
    m = jnp.mean(x, axis=axis, keepdims=True)
    v = jnp.var(x, axis=axis, keepdims=True)
    return (x - m) / jnp.sqrt(v + eps)

def _scatter_add(tgt, idx, src, axis=0):
    return tgt.at[idx].add(src)

def _segment_sum(src, seg, n):
    return jax.ops.segment_sum(src, seg, n)
kernel_name = 'mk_gnn_resnorm_d2_gnn_r8_10e588'

def setup_inputs(seed: int=0):
    np.random.seed(seed)
    _w = jnp.asarray

    def _rec_inputs():
        import jax
        import jax.numpy as jnp
        _gk = jax.random.key(seed)
        x = -8.776e-05 + 1 * jax.random.normal(jax.random.fold_in(_gk, 1), (2500, 256), jnp.float32)
        _s = jax.random.randint(jax.random.fold_in(_gk, 2), (40000,), 0, 2500, jnp.int32)
        _d = jax.random.randint(jax.random.fold_in(_gk, 3), (40000,), 0, 2500, jnp.int32)
        _loop = jnp.arange(2500, dtype=jnp.int32)
        src = jnp.concatenate([_s, _d, _loop])
        dst = jnp.concatenate([_d, _s, _loop])
        _o = jnp.argsort(dst, stable=True)
        src = src[_o]
        dst = dst[_o]
        edge_type_8 = jax.random.randint(jax.random.fold_in(_gk, 13), (82500,), 0, 8, jnp.int32)
        edge_weight1 = jax.random.uniform(jax.random.fold_in(_gk, 14), (82500, 1), jnp.float32, 0.0, 0.999994)
        return (x, src, dst, edge_type_8, edge_weight1)
    x, src, dst, edge_type_8, edge_weight1 = _rec_inputs()

    def _L0_gnn_setup():
        import jax, jax.numpy as jnp
        import numpy as np
        N_NODES = 2500
        N_EDGES = 40000
        D = 256
        R = 8
        B = 8
        L = 2
        key = jax.random.key(seed)
        ks = jax.random.split(key, 8)
        feat = jax.random.normal(ks[0], (N_NODES, D), dtype=jnp.float32)
        norm = jax.random.uniform(ks[1], (N_EDGES, 1), dtype=jnp.float32)
        basis = jax.random.normal(ks[2], (L, B, D, D), dtype=jnp.float32) * 0.02
        coeff = jax.random.normal(ks[3], (L, R, B), dtype=jnp.float32)
        bias = jnp.zeros((L, D), dtype=jnp.float32)
        src = jax.random.randint(ks[4], (N_EDGES,), 0, N_NODES, dtype=jnp.int32)
        dst = jax.random.randint(ks[5], (N_EDGES,), 0, N_NODES, dtype=jnp.int32)
        etype = jax.random.randint(ks[6], (N_EDGES,), 0, R, dtype=jnp.int32)
        return {'feat': feat, 'norm': norm, 'basis': basis, 'coeff': coeff, 'bias': bias, 'src': src, 'dst': dst, 'etype': etype}
    _L0_gnn_all = _L0_gnn_setup()
    _L0_gnn_in = {k: v for k, v in _L0_gnn_all.items() if k in ('basis', 'coeff', 'bias')}
    del _L0_gnn_all

    def _L1_gnn_setup():
        import jax, jax.numpy as jnp
        import numpy as np
        N_NODES = 6250
        N_EDGES = 100000
        IN_CH = 256
        HID_CH = 256
        OUT_CH = 256
        N_LAYERS = 3
        key = jax.random.key(seed)
        ks = jax.random.split(key, 8)
        s_in = 1.0 / np.sqrt(IN_CH)
        s_h = 1.0 / np.sqrt(HID_CH)
        return {'x': jax.random.normal(ks[0], (N_NODES, IN_CH), dtype=jnp.float32), 'W_in': jax.random.normal(ks[1], (IN_CH, HID_CH), dtype=jnp.float32) * s_in, 'b_in': jnp.zeros((HID_CH,), dtype=jnp.float32), 'W_agg': jax.random.normal(ks[2], (N_LAYERS, HID_CH, HID_CH), dtype=jnp.float32) * s_h, 'W_self': jax.random.normal(ks[3], (N_LAYERS, HID_CH, HID_CH), dtype=jnp.float32) * s_h, 'b_hid': jnp.zeros((N_LAYERS, HID_CH), dtype=jnp.float32), 'W_out': jax.random.normal(ks[4], (HID_CH, OUT_CH), dtype=jnp.float32) * s_h, 'b_out': jnp.zeros((OUT_CH,), dtype=jnp.float32), 'edge_index': jax.random.randint(ks[5], (2, N_EDGES), 0, N_NODES, dtype=jnp.int64)}
    _L1_gnn_all = _L1_gnn_setup()
    _L1_gnn_in = {k: v for k, v in _L1_gnn_all.items() if k in ('W_in', 'b_in', 'W_agg', 'W_self', 'b_hid', 'W_out', 'b_out')}
    del _L1_gnn_all
    return {'x': x, 'src': src, 'dst': dst, 'edge_type_8': edge_type_8, 'edge_weight1': edge_weight1, 'L0_gnn_basis': _L0_gnn_in['basis'], 'L0_gnn_coeff': _L0_gnn_in['coeff'], 'L0_gnn_bias': _L0_gnn_in['bias'], 'L1_gnn_W_in': _L1_gnn_in['W_in'], 'L1_gnn_b_in': _L1_gnn_in['b_in'], 'L1_gnn_W_agg': _L1_gnn_in['W_agg'], 'L1_gnn_W_self': _L1_gnn_in['W_self'], 'L1_gnn_b_hid': _L1_gnn_in['b_hid'], 'L1_gnn_W_out': _L1_gnn_in['W_out'], 'L1_gnn_b_out': _L1_gnn_in['b_out']}

def reference(x, src, dst, edge_type_8, edge_weight1, L0_gnn_basis, L0_gnn_coeff, L0_gnn_bias, L1_gnn_W_in, L1_gnn_b_in, L1_gnn_W_agg, L1_gnn_W_self, L1_gnn_b_hid, L1_gnn_W_out, L1_gnn_b_out):
    import jax
    import jax.numpy as jnp

    def _L0_gnn_ref(feat, norm, basis, coeff, bias, src, dst, etype):
        import jax, jax.numpy as jnp
        import numpy as np
        N_NODES = 2500
        N_EDGES = 40000
        D = 256
        R = 8
        B = 8
        L = 2
        'Stacked RelGraphConv (basis regularizer, self_loop=False, bias=True),\n            ReLU between layers, none after the last layer.'
        h = feat
        for l in range(L):
            W = jnp.einsum('rb,bio->rio', coeff[l], basis[l])
            all_h = jnp.einsum('ni,rio->rno', h, W)
            msg = all_h[etype, src] * norm
            agg = jax.ops.segment_sum(msg, dst, num_segments=N_NODES)
            h = agg + bias[l]
            if l < L - 1:
                h = jax.nn.relu(h)
        return h

    def _L1_gnn_ref(x, W_in, b_in, W_agg, W_self, b_hid, W_out, b_out, edge_index):
        import jax, jax.numpy as jnp
        import numpy as np
        N_NODES = 6250
        N_EDGES = 100000
        IN_CH = 256
        HID_CH = 256
        OUT_CH = 256
        N_LAYERS = 3
        n = x.shape[0]
        dst = edge_index[0]
        src = edge_index[1]
        n_layers = W_agg.shape[0]
        h = x @ W_in + b_in
        deg = jax.ops.segment_sum(jnp.ones_like(dst, dtype=h.dtype), dst, num_segments=n)
        deg = jnp.maximum(deg, 1.0)[:, None]
        for l in range(n_layers):
            agg = jax.ops.segment_sum(h[src], dst, num_segments=n) / deg
            h = jax.nn.relu(agg @ W_agg[l] + h @ W_self[l] + b_hid[l])
        return h @ W_out + b_out
    edge_index = jnp.stack([src, dst])
    x = _layernorm(x + _L0_gnn_ref(x, edge_weight1, L0_gnn_basis, L0_gnn_coeff, L0_gnn_bias, src, dst, edge_type_8), axis=-1)
    x = _layernorm(x + _L1_gnn_ref(x, L1_gnn_W_in, L1_gnn_b_in, L1_gnn_W_agg, L1_gnn_W_self, L1_gnn_b_hid, L1_gnn_W_out, L1_gnn_b_out, edge_index), axis=-1)
    return x

_drawn_inputs = setup_inputs


def setup_inputs(seed=0):
    import zlib

    import numpy as np

    out = dict(_drawn_inputs(seed))
    spreads = {'L0_gnn_bias': (0.0, 0.267),
     'L1_gnn_b_in': (0.0, 0.1),
     'L1_gnn_b_hid': (0.0, 0.1),
     'L1_gnn_b_out': (0.0, 0.1)}
    factors = {}
    for name, (base, spread) in spreads.items():
        noise = np.random.default_rng([zlib.crc32(name.encode()), seed]).standard_normal(out[name].shape)
        drawn = base * np.exp(spread * noise) if base else spread * noise
        out[name] = jnp.asarray(drawn.astype(out[name].dtype))
    for name, factor in factors.items():
        out[name] = (out[name] * factor).astype(out[name].dtype)
    return out
```

```python
from contextlib import ExitStack

import concourse.bass as bass
from concourse import mybir

F32 = mybir.dt.float32
BF16 = mybir.dt.bfloat16
F16 = mybir.dt.float16
I32 = mybir.dt.int32
ALU = mybir.AluOpType
ACT = mybir.ActivationFunctionType
AX = mybir.AxisListType.X
RMAX = bass.bass_isa.ReduceOp.max

N = 2500
D = 256
E = 82500
R = 8
T = 645
LASTP = E - (T - 1) * 128
TW = 29
NW = 23
TA = 3
NA = 215
NB = 320
NS = 8 * NB
JB = 20
PB = 125
CH = 500
NC = 5
NG = 16
NSL = 8
EPS = 1e-5


class Queues:

    def __init__(self, sems):
        self.ops = {e: [] for e in ("pe", "act", "dve", "pool", "sp")}
        self.sems = sems
        self.n = {}
        self.seen = {}

    def wait(self, eng, *events):
        for ev in events:
            if ev is None:
                continue
            sem, v = ev
            if self.seen.get((eng, sem), 0) < v:
                self.seen[(eng, sem)] = v
                self.ops[eng].append(lambda e, s=self.sems[sem], v=v: e.wait_ge(s, v))

    def op(self, eng, fn, *events, sig=True):
        self.wait(eng, *events)
        if not sig:
            self.ops[eng].append(fn)
            return None
        s = self.sems[eng]
        self.ops[eng].append(lambda e: fn(e).then_inc(s, 1))
        self.n[eng] = self.n.get(eng, 0) + 1
        return eng, self.n[eng]

    def dma(self, eng, fn, sem, *events):
        self.wait(eng, *events)
        s = self.sems[sem]
        self.ops[eng].append(lambda e: fn(e).then_inc(s, 16))
        self.n[sem] = self.n.get(sem, 0) + 16
        return sem, self.n[sem]


class Names:
    pass


class Relay:

    def __init__(self, sems):
        self.sems = sems
        self.top = []
        self.at = [self.top]

    def step(self, eng, fn):
        self.at[-1].append((eng, fn))

    def loop(self, name, count, fill):
        body = []
        self.at[-1].append((None, name, count, body))
        self.at.append(body)
        fill()
        self.at.pop()

    def first(self, item):
        return item[0] or self.first(item[3][0])

    def engines(self, body):
        got = set()
        for item in body:
            got |= {item[0]} if item[0] else self.engines(item[3])
        return got

    def emit(self, eng, e, body, after, v):
        for n, item in enumerate(body):
            nxt = self.first(body[n + 1]) if n + 1 < len(body) else after
            if item[0] is None:
                _, name, count, inner = item
                assert nxt in (None, self.first(inner[0]))
                if eng in self.engines(inner):
                    with e.Fori(0, count) as i:
                        self.emit(eng, e, inner, self.first(inner[0]), {**v, name: i})
            elif item[0] == eng:
                own = self.sems["k_" + eng]
                e.wait_ge(own, 1)
                e.sem_clear(own)
                give = self.sems["k_" + (nxt or "end")]
                if eng == "sp":
                    item[1](e, v).then_inc(self.sems["k_dma"], 16)
                    e.wait_ge(self.sems["k_dma"], 16)
                    e.sem_clear(self.sems["k_dma"])
                    e.sem_inc(give, 1)
                elif eng == "pool":
                    item[1](e, v).then_inc(self.sems["k_gather"], 16)
                    e.drain().then_inc(give, 1)
                else:
                    item[1](e, v).then_inc(give, 1)


def general(relay, m):
    dve, act, pe, sp, pool = (lambda fn, g=g: relay.step(g, fn) for g in ("dve", "act", "pe", "sp", "pool"))

    def rows(ap, v):
        return ap[bass.ds(v["k"] * PB, PB), :]

    def sums(table, index, key, weight):
        dve(lambda e, v: e.memset(m.acc, 0.0))

        def tile():
            dve(lambda e, v: e.tensor_copy(m.ix, index[:, bass.ds(v["t"], 1)]))
            dve(lambda e, v: e.tensor_copy(m.dw[:, 0:1], key[:, bass.ds(v["t"], 1)]))
            dve(lambda e, v: e.tensor_copy(m.dw[:, 1:2], weight[:, bass.ds(v["t"], 1)]))
            dve(lambda e, v: e.tensor_tensor(m.dw[:, 0:1], m.dw[:, 0:1], m.base, ALU.subtract))
            dve(lambda e, v: e.tensor_scalar(m.S, m.iot, m.dw[:, 0:1], m.dw[:, 1:2], ALU.is_equal, ALU.mult))
            pool(lambda e, v: e.indirect_dma_start(m.G, None, table, bass.IndirectOffsetOnAxis(ap=m.ix, axis=0)))
            pe(lambda e, v: e.matmul(m.bank[0][:, 0:256], m.S, m.G, start=True, stop=True))
            pe(lambda e, v: e.matmul(m.bank[1][:, 0:1], m.S, m.onef, start=True, stop=True))
            dve(lambda e, v: e.tensor_tensor(m.acc[:, 0:256], m.acc[:, 0:256], m.bank[0][:, 0:256], ALU.add))
            dve(lambda e, v: e.tensor_tensor(m.acc[:, 256:257], m.acc[:, 256:257], m.bank[1][:, 0:1], ALU.add))

        relay.loop("t", T, tile)

    def turned(src, dst):
        for k in range(2):
            pe(lambda e, v, k=k: e.transpose(m.bank[2][:, k * 128:k * 128 + PB], src[0:PB, k * 128:(k + 1) * 128], m.idn[0:PB, 0:PB]))
        act(lambda e, v: e.copy(dst[:, :, 0:PB], m.bank[2][:, 0:256].rearrange("p (k n) -> p k n", n=128)[:, :, 0:PB]))

    def product(pairs, cols=256):
        n = 2 * len(pairs)
        for i, (hT_, w_) in enumerate(pairs):
            for k in range(2):
                pe(lambda e, v, hT_=hT_, w_=w_, k=k, i=i: e.matmul(m.bank[3][0:PB, 0:cols], hT_[:, k, 0:PB], w_[:, k, :],
                                                                   start=(i == 0 and k == 0), stop=(2 * i + k == n - 1)))

    def norm(y, o):
        dve(lambda e, v: e.bn_stats(m.st[0:PB, 0, :], y[0:PB, :]))
        dve(lambda e, v: e.bn_aggr(m.sm[0:PB, 0, 0:2], m.st[0:PB, 0, :]))
        act(lambda e, v: e.activation(m.sm[0:PB, 0, 2:3], m.sm[0:PB, 0, 1:2], ACT.Sqrt, bias=m.eps[0:PB, 0:1]))
        dve(lambda e, v: e.reciprocal(m.sm[0:PB, 0, 3:4], m.sm[0:PB, 0, 2:3]))
        dve(lambda e, v: e.tensor_scalar(o[0:PB, :], y[0:PB, :], m.sm[0:PB, 0, 0:1], m.sm[0:PB, 0, 3:4], ALU.subtract, ALU.mult))

    def blocks(fill):
        dve(lambda e, v: e.memset(m.base, 0.0))

        def body():
            fill()
            dve(lambda e, v: e.tensor_scalar(m.base, m.base, float(PB), None, ALU.add))
        relay.loop("k", JB, body)

    def first():
        sums(m.T1g, m.idx, m.df, m.wgt)
        dve(lambda e, v: e.tensor_tensor(m.y, m.acc[:, 0:256], m.b1, ALU.add))
        dve(lambda e, v: e.tensor_scalar(m.y, m.y, 0.0, None, ALU.max))
        turned(m.y, m.hT)
        for c in range(4):
            product([(m.hT, m.W2[:, :, c * 512:(c + 1) * 512])], 512)
            act(lambda e, v, c=c: e.copy(m.row[0:PB, c * 512:(c + 1) * 512], m.bank[3][0:PB, :]))
        sp(lambda e, v: e.dma_start(rows(m.T2, v), m.row[0:PB, :]))

    def second():
        sums(m.T2g, m.idx, m.df, m.wgt)
        dve(lambda e, v: e.tensor_tensor(m.y, m.acc[:, 0:256], m.b2, ALU.add))
        sp(lambda e, v: e.dma_start(m.z[0:PB, :], rows(m.x, v)))
        dve(lambda e, v: e.tensor_tensor(m.y[0:PB, :], m.y[0:PB, :], m.z[0:PB, :], ALU.add))
        norm(m.y, m.z)
        sp(lambda e, v: e.dma_start(rows(m.X1, v), m.z[0:PB, :]))
        turned(m.z, m.hT)
        product([(m.hT, m.wts[:, 0, :, :])])
        dve(lambda e, v: e.tensor_tensor(m.y[0:PB, :], m.bank[3][0:PB, 0:256], m.brow4[0:PB, 0, :], ALU.add))
        sp(lambda e, v: e.dma_start(rows(m.H[0], v), m.y[0:PB, :]))

    def sage(l):
        def f():
            sums(m.H[l], m.di, m.sf, m.wone)
            dve(lambda e, v: e.tensor_scalar(m.acc[:, 256:257], m.acc[:, 256:257], 1.0, None, ALU.max))
            sp(lambda e, v: e.dma_start(m.z[0:PB, :], rows(m.H[l], v)))
            dve(lambda e, v: e.reciprocal(m.acc[:, 256:257], m.acc[:, 256:257]))
            dve(lambda e, v: e.tensor_scalar(m.y, m.acc[:, 0:256], m.acc[:, 256:257], None, ALU.mult))
            turned(m.y, m.hT)
            turned(m.z, m.hT2)
            product([(m.hT, m.wts[:, 1 + 2 * l, :, :]), (m.hT2, m.wts[:, 2 + 2 * l, :, :])])
            dve(lambda e, v: e.tensor_tensor(m.y[0:PB, :], m.bank[3][0:PB, 0:256], m.brow4[0:PB, 1 + l, :], ALU.add))
            dve(lambda e, v: e.tensor_scalar(m.y, m.y, 0.0, None, ALU.max))
            sp(lambda e, v: e.dma_start(rows(m.H[l + 1], v), m.y[0:PB, :]))
        return f

    def last():
        sp(lambda e, v: e.dma_start(m.z[0:PB, :], rows(m.H[3], v)))
        turned(m.z, m.hT)
        product([(m.hT, m.wts[:, 7, :, :])])
        sp(lambda e, v: e.dma_start(m.z[0:PB, :], rows(m.X1, v)))
        dve(lambda e, v: e.tensor_tensor(m.y[0:PB, :], m.bank[3][0:PB, 0:256], m.bo[0:PB, :], ALU.add))
        dve(lambda e, v: e.tensor_tensor(m.y[0:PB, :], m.y[0:PB, :], m.z[0:PB, :], ALU.add))
        norm(m.y, m.z)
        sp(lambda e, v: e.dma_start(rows(m.out, v), m.z[0:PB, :]))

    dve(lambda e, v: e.memset(m.onef, 1.0))
    sp(lambda e, v: e.dma_start(m.brow, m.b_rows.to_broadcast([128, 4 * D])))
    dve(lambda e, v: e.memset(m.wone, 1.0))
    dve(lambda e, v: e.tensor_scalar(m.wone[:, T - 1:T], m.ip, float(LASTP), None, ALU.is_lt))
    for f in (first, second, sage(0), sage(1), sage(2)):
        blocks(f)
    dve(lambda e, v: e.memset(m.base, 0.0))

    def body():
        dve(lambda e, v: e.memset(m.base, 0.0))
        last()
    relay.loop("k", JB, body)
    dve(lambda e, v: e.memset(m.base, 0.0))


def program(nc, x, srcT, dstT, etT, wT, first, first2, basis, coeff, bias, W_in, b_in, W_agg, W_self,
            b_rows, W_out, b_out, out):
    T1 = nc.dram_tensor("T1", (N, R * D), F32, kind="Internal").ap()
    T2 = nc.dram_tensor("T2", (N, R * D), F32, kind="Internal").ap()
    Ad = nc.dram_tensor("Ad", (N, NS), BF16, kind="Internal").ap()
    X1 = nc.dram_tensor("X1", (N, D), F32, kind="Internal").ap()
    H = [nc.dram_tensor(f"H{i}", (N, D), F32, kind="Internal").ap() for i in range(4)]

    with ExitStack() as ctx:
        def sb(n, s, d):
            return ctx.enter_context(nc.sbuf_tensor(n, s, d))

        def ps(n, s, d=F32):
            return ctx.enter_context(nc.psum_tensor(n, s, d))

        names = (["pe", "act", "dve", "pool"]
                 + [f"g{i}" for i in range(NG)] + ["in", "bas0", "bas1", "xin", "wts", "t1a", "t1b", "t2a", "t2b", "aw",
                 "k_pe", "k_act", "k_dve", "k_pool", "k_sp", "k_end", "k_dma", "k_gather", "xw0", "xw1", "x1", "ar0", "ar1", "xs0", "xs1", "o0", "o1"])
        sems = {n: ctx.enter_context(nc.semaphore("s_" + n)) for n in names}
        Q = Queues(sems)
        op, dma = Q.op, Q.dma

        RA = sb("RA", [128, 25600], F32)
        RB = sb("RB", [128, 17920], F32)

        def view(reg, off, shape, dt):
            size = {F32: 4, I32: 4, BF16: 2, F16: 2}[dt]
            n = 1
            for s in shape:
                n *= s
            nb = n * size
            assert off % 4 == 0 and off + nb <= reg.shape[1] * 4, (off, nb)
            v = reg[:, off // 4:(off + nb + 3) // 4]
            if dt != F32:
                v = v.bitcast(dt)
            v = v[:, 0:n]
            if len(shape) == 2:
                v = v.rearrange("p (a b) -> p a b", b=shape[1])
            elif len(shape) == 3:
                v = v.rearrange("p (a b c) -> p a b c", b=shape[1], c=shape[2])
            return v

        def lay(reg, *items):
            off, got = 0, []
            for shape, dt in items:
                got.append(view(reg, off, shape, dt))
                n = {F32: 4, I32: 4, BF16: 2, F16: 2}[dt]
                for s in shape:
                    n *= s
                off += (n + 31) // 32 * 32
            return got

        W1, W2, bas, tb, rowb, xs = lay(RA, ((2, 2048), F32), ((2, 2048), F32), ((8, 2, 256), F32),
                                        ((2, 4 * 512), F32), ((2, 2048), F32), ((20, 256), F32))
        tb = tb.rearrange("p s (q c) -> p s q c", c=512)
        A_sb = view(RA, 0, (20, N), BF16)
        (G, S, Pg, hw, hTw, Ew, Mr, Nr, Aw, E2, c1, bcol, xw, x1w) = lay(
            RB, ((NG, 256), F32), ((NSL, 128), F32), ((2, 256), F32), ((2, 256), F32), ((2, 256), F32),
            ((2, 128), F32), ((NSL, 128), BF16), ((NSL, NB), BF16), ((4, NB), BF16), ((2, 128), BF16),
            ((T,), F32), ((T,), F32), ((2, 256), F32), ((2, 256), F32))
        xT = view(RB, 0, (2, N), F32)
        hs, hT, agT, rdeg = lay(RB, ((20, 3 * 256), BF16), ((2, N), F32), ((2, 1000), F32), ((N,), F32))
        hs = hs.rearrange("p j (q c) -> p j q c", c=256)
        agT = agT.rearrange("p s (k c) -> p s k c", c=CH)

        wts = sb("wts", [128, 8, 2, 256], F32)
        idn = sb("idn", [128, 128], F32)
        ones = sb("ones", [128, 128], BF16)
        iot = sb("iot", [128, 128], F32)
        iotN = sb("iotN", [128, NB], F16)
        ip = sb("ip", [128, 1], F32)
        b1 = sb("b1", [128, 256], F32)
        b2 = sb("b2", [128, 256], F32)
        bo = sb("bo", [128, 256], F32)
        bT = sb("bT", [128, 8], F32)
        eps = sb("eps", [128, 1], F32)
        cf = sb("cf", [128, 128], F32)
        dl = sb("dl", [128, T], F32)
        wgt = sb("wgt", [128, T], F32)
        idx = sb("idx", [128, T], I32)
        ba = sb("ba", [128, NW], F32)
        ba2 = sb("ba2", [128, NA], F32)
        bai = sb("bai", [128, NW], I32)
        ba2i = sb("ba2i", [128, NA], I32)
        pd1 = sb("pd1", [128, NW], F32)
        pd2 = sb("pd2", [128, NA], F32)
        chk = sb("chk", [128, 16], F32)
        flag = sb("flag", [128, 1], I32)
        st = sb("st", [128, 2, 6], F32)
        sm = sb("sm", [128, 2, 4], F32)

        si, di, ei, sf, df, ef, aq = lay(RB[:, 43072 // 4:17920], *[((T,), d) for d in (I32, I32, I32, F32, F32, F32, F32)])

        bank = [ps(f"bank{i}", [128, 512]) for i in range(8)]

        ld = dma("sp", lambda e: e.dma_start(di, dstT), "in")
        ld = dma("sp", lambda e: e.dma_start(si, srcT), "in")
        ld = dma("sp", lambda e: e.dma_start(ei, etT), "in")
        ld = dma("sp", lambda e: e.dma_start(wgt[:, :], wT), "in")
        ld = dma("sp", lambda e: e.dma_start(bai[:, :], first.to_broadcast([128, NW])), "in")
        ld = dma("sp", lambda e: e.dma_start(ba2i[:, :], first2.to_broadcast([128, NA])), "in")
        ldx = dma("act", lambda e: e.dma_start(xs[0:PB, :, :], x.rearrange("(j p) f -> p j f", p=PB)), "xin")
        ldb = [None, None]
        dma("act", lambda e: e.dma_start(cf[:, :], coeff.to_broadcast([128, 128])), "bas0")
        ldb[0] = dma("act", lambda e: e.dma_start(bas, basis[0].rearrange("b (k p) o -> p b k o", p=128)), "bas0")
        for i, w in enumerate([W_in, W_agg[0], W_self[0], W_agg[1], W_self[1], W_agg[2], W_self[2], W_out]):
            ldw = dma("sp", lambda e, i=i, w=w: e.dma_start(wts[:, i, :, :], w.rearrange("(k p) o -> p k o", p=128)), "wts")
        for t_, s_ in ((b1, bias[0:1, :]), (b2, bias[1:2, :]), (bo, b_out)):
            ldw = dma("sp", lambda e, t_=t_, s_=s_: e.dma_start(t_[:, :], s_.to_broadcast([128, 256])), "wts")
        ldw = dma("sp", lambda e: e.dma_start(bT[:, :], b_in), "wts")

        e1 = op("pool", lambda e: e.iota(iot[:, :], pattern=[[1, 128]], base=0, channel_multiplier=0,
                                         allow_small_or_imprecise_dtypes=True))
        e2 = op("pool", lambda e: e.iota(ip[:, :], pattern=[[1, 1]], base=0, channel_multiplier=1,
                                         allow_small_or_imprecise_dtypes=True))
        e3 = op("pool", lambda e: e.iota(iotN[:, :], pattern=[[1, NB]], base=0, channel_multiplier=0,
                                         allow_small_or_imprecise_dtypes=True))
        op("dve", lambda e: e.memset(ones[:, :], 1.0))
        op("dve", lambda e: e.memset(eps[:, :], EPS))
        cid = op("dve", lambda e: e.tensor_scalar(idn[:, :], iot[:, :], ip[:, 0:1], None, ALU.is_equal), e3)

        xT_done = []
        tr_free = [None, None]
        for j in range(JB):
            b = bank[6 + j % 2]
            Q.wait("pe", cid, ldx, tr_free[j % 2])
            for k in range(2):
                ev = op("pe", lambda e, b=b, j=j, k=k: e.transpose(b[:, k * 128:k * 128 + PB], xs[0:PB, j, k * 128:(k + 1) * 128],
                                                                   idn[0:PB, 0:PB]), sig=(k == 1))
            src_ = b[:, 0:256].rearrange("p (k n) -> p k n", n=128)[:, :, 0:PB]
            ev = op("act", lambda e, j=j, s=src_: e.copy(xT[:, :, j * PB:(j + 1) * PB], s), ev)
            tr_free[j % 2] = ev
            xT_done.append(ev)

        def relation_weights(l, W, pair):
            last = [None, None]
            for b in range(8):
                for q in range(2):
                    r = 2 * pair + q
                    o = W[:, :, r * 256:(r + 1) * 256]
                    c = cf[:, l * 64 + r * 8 + b:l * 64 + r * 8 + b + 1]
                    if b == 0:
                        last[q] = op("dve", lambda e, o=o, c=c, b=b: e.tensor_scalar(o, bas[:, b, :, :], c, None, ALU.mult), ldb[l])
                    else:
                        last[q] = op("dve", lambda e, o=o, c=c, b=b: e.scalar_tensor_tensor(o, bas[:, b, :, :], c, o, ALU.mult, ALU.add),
                                     last[q])
            return last[1]

        W1_done = [relation_weights(0, W1, p) for p in range(4)]

        def pool(fn, *ev):
            return op("pool", fn, *ev)

        Q.wait("pool", ld)
        ev = pool(lambda e: e.tensor_copy(df, di))
        ev = pool(lambda e: e.tensor_copy(sf, si))
        ev = pool(lambda e: e.tensor_copy(ef, ei))
        ev = pool(lambda e: e.tensor_copy(ba[:, :], bai[:, :]))
        ev = pool(lambda e: e.tensor_copy(ba2[:, :], ba2i[:, :]))
        ev = pool(lambda e: e.tensor_scalar(ba[:, :], ba[:, :], float(N - 128), None, ALU.min), ev)
        ev = pool(lambda e: e.tensor_scalar(ba2[:, :], ba2[:, :], float(N - 16), None, ALU.min), ev)
        pool(lambda e: e.memset(ba[:, 0:1], 0.0), ev)
        pool(lambda e: e.memset(ba[:, NW - 1:NW], float(N - 128)), ev)
        pool(lambda e: e.memset(ba2[:, 0:1], 0.0), ev)
        ev = pool(lambda e: e.memset(ba2[:, NA - 1:NA], float(N - 16)), ev)
        eb = pool(lambda e: e.tensor_copy(bai[:, :], ba[:, :]), ev)
        ev = pool(lambda e: e.tensor_scalar(pd2[:, :], ba2[:, :], 8.0, None, ALU.mult), ev)
        base_done = pool(lambda e: e.tensor_copy(ba2i[:, :], pd2[:, :]), ev)
        ev = pool(lambda e: e.tensor_scalar(aq, sf, 8.0, None, ALU.mult))
        ev = pool(lambda e: e.tensor_tensor(aq, aq, ef, ALU.add), ev)
        idx_done = pool(lambda e: e.tensor_copy(idx[:, :], aq), ev)
        nf = (NW - 1) * TW
        pool(lambda e: e.tensor_tensor(dl[:, 0:nf].rearrange("p (w t) -> p w t", t=TW),
                                       df[:, 0:nf].rearrange("p (w t) -> p w t", t=TW),
                                       ba[:, 0:NW - 1].unsqueeze(2).to_broadcast([128, NW - 1, TW]), ALU.subtract), eb)
        dl_done = pool(lambda e: e.tensor_scalar(dl[:, nf:T], df[:, nf:T], ba[:, NW - 1:NW], None, ALU.subtract))
        ev = pool(lambda e: e.tensor_tensor(c1.rearrange("p (w t) -> p w t", t=TA), df.rearrange("p (w t) -> p w t", t=TA),
                                            ba2[:, :].unsqueeze(2).to_broadcast([128, NA, TA]), ALU.subtract))
        dl2_done = ev
        pool(lambda e: e.tensor_tensor(pd1[:, 1:NW], ba[:, 1:NW], ba[:, 0:NW - 1], ALU.subtract))
        dp = pool(lambda e: e.tensor_tensor(pd2[:, 1:NA], ba2[:, 1:NA], ba2[:, 0:NA - 1], ALU.subtract), base_done)

        def check(col, src_, sign, lim, *ev):
            a = op("dve", lambda e: e.tensor_reduce(chk[:, col:col + 1], src_, AX, ALU.max if sign > 0 else ALU.min), *ev)
            return op("dve", lambda e: e.tensor_scalar(chk[:, col:col + 1], chk[:, col:col + 1], float(sign), float(lim),
                                                       ALU.mult, ALU.add), a)

        check(0, dl[:, :], -1, 0, dl_done)
        check(1, dl[:, :], 1, -127)
        check(2, c1, -1, 0, dl2_done)
        ck3 = check(3, c1, 1, -15)
        check(4, pd1[:, 1:NW], -1, 0, dp)
        check(5, pd1[:, 1:NW], 1, -128)
        check(6, pd2[:, 1:NA], -1, 0)
        ck7 = check(7, pd2[:, 1:NA], 1, -16)
        ev = op("dve", lambda e: e.tensor_tensor(ef[:, 0:T - 2], df[:, 2:T], df[:, 0:T - 2], ALU.subtract), idx_done)
        ck8 = check(8, ef[:, 0:T - 2], -1, 1, ev)
        ev = op("dve", lambda e: e.tensor_reduce(chk[:, 9:10], chk[:, 0:9], AX, ALU.max), ck8)
        ev = op("pool", lambda e: e.partition_all_reduce(chk[:, 10:11], chk[:, 9:10], 128, RMAX), ev)
        flag_done = op("dve", lambda e: e.tensor_scalar(flag[:, :], chk[:, 10:11], 0.0, None, ALU.is_le), ev)

        pool(lambda e: e.tensor_scalar(pd1[:, 1:NW], pd1[:, 1:NW], -1.0, None, ALU.mult), ck7)
        ev = pool(lambda e: e.tensor_scalar(pd2[:, 1:NA], pd2[:, 1:NA], -8.0, None, ALU.mult))
        pool(lambda e: e.tensor_scalar(pd1[:, 1:NW], pd1[:, 1:NW], ip[:, 0:1], None, ALU.add), ev)
        pd_done = pool(lambda e: e.tensor_scalar(pd2[:, 1:NA], pd2[:, 1:NA], ip[:, 0:1], None, ALU.add))
        ev = pool(lambda e: e.tensor_scalar(c1, c1, 8.0, None, ALU.mult), ck3)
        ev2 = pool(lambda e: e.tensor_scalar(bcol, sf, 1.0, None, ALU.mult))
        for q in range(1, 8):
            ev = pool(lambda e, q=q: e.tensor_scalar(aq, sf, float(NB * q), None, ALU.is_ge), ev)
            ev2 = pool(lambda e, q=q: e.tensor_tensor(c1, c1, aq, ALU.add), ev)
            ev = pool(lambda e, q=q: e.tensor_scalar(ef, aq, float(-NB), None, ALU.mult), ck8)
            ev = pool(lambda e, q=q: e.tensor_tensor(bcol, bcol, ef, ALU.add), ev, ev2)
        code_done = ev

        tb_free = [None, None]
        bk_free = [None] * 2
        nb_ = 0
        tdma = ["t1a", "t1b"]
        tab_done = []
        evac = 0
        for p in range(4):
            for q in range(5):
                s = (p * 5 + q) % 2
                evs = []
                for jj in range(4):
                    j = 4 * q + jj
                    b = 4 + nb_ % 2
                    Q.wait("pe", W1_done[p], xT_done[j], bk_free[nb_ % 2])
                    for k in range(2):
                        ev = op("pe", lambda e, b=b, j=j, k=k, p=p: e.matmul(
                            bank[b][0:PB, :], xT[:, k, j * PB:(j + 1) * PB], W1[:, k, p * 512:(p + 1) * 512],
                            start=(k == 0), stop=(k == 1)), sig=(k == 1))
                    last_mm = ev
                    o = tb[0:PB, s, jj, :]
                    i_ = bank[b][0:PB, :]
                    ev = op("act", lambda e, o=o, i_=i_: e.copy(o, i_), ev, tb_free[s])
                    bk_free[nb_ % 2] = ev
                    evs.append(ev)
                    nb_ += 1
                dst_ = T1.rearrange("(j p) c -> p j c", p=PB)[:, 4 * q:4 * q + 4, p * 512:(p + 1) * 512]
                tb_free[s] = dma("sp", lambda e, d=dst_, s=s: e.dma_start(d, tb[0:PB, s, :, :]), tdma[s], *evs)
                tab_done = [tb_free[0], tb_free[1]]
        table1_done = [x for x in tab_done if x]
        xT_read = last_mm

        ldb[1] = dma("act", lambda e: e.dma_start(bas, basis[1].rearrange("b (k p) o -> p b k o", p=128)), "bas1", W1_done[3])
        W2_done = [relation_weights(1, W2, p) for p in range(4)][3]

        all_done = [("pe", Q.n["pe"]), ("act", Q.n["act"]), ("pool", Q.n["pool"]), ("dve", Q.n["dve"]),
                    *table1_done, ldw, ldx, ld, ldb[1]]
        head = {k: len(v) for k, v in Q.ops.items()}
        m = Names()
        m.T1g = T1.rearrange("n (r o) -> (n r) o", o=D)
        m.T2g = T2.rearrange("n (r o) -> (n r) o", o=D)
        m.T2 = T2
        m.X1 = X1
        m.H = H
        m.x = x
        m.out = out
        m.idx = idx
        m.wgt = wgt
        m.di = di
        m.df = df
        m.sf = sf
        m.ip = ip[:, :]
        m.iot = iot[:, :]
        m.idn = idn
        m.b1 = b1[:, :]
        m.b2 = b2[:, :]
        m.bo = bo
        m.W2 = W2
        m.wts = wts
        m.row = rowb[:, 0, :]
        m.st = st
        m.sm = sm
        m.eps = eps
        m.bank = bank
        m.b_rows = b_rows
        (m.G, m.S, m.acc, m.y, m.z, m.hT, m.hT2, m.wone, brow, m.dw, m.onef, m.ix, m.base) = lay(
            RB[:, 0:43072 // 4], ((256,), F32), ((128,), F32), ((257,), F32), ((256,), F32), ((256,), F32), ((2, 128), F32),
            ((2, 128), F32), ((T,), F32), ((4 * D,), F32), ((2,), F32), ((1,), F32), ((1,), I32), ((1,), F32))
        m.brow = brow
        relay = Relay(sems)
        m.brow4 = brow.rearrange("p (l c) -> p l c", c=D)
        general(relay, m)

        T1g = T1.rearrange("n (r o) -> (n r) o", o=D)
        T2g = T2.rearrange("n (r o) -> (n r) o", o=D)
        Adw = Ad.rearrange("d (a b) -> (d a) b", b=NB)

        g_read = [None] * NG
        s_read = [xT_read] * NSL
        m_read = [None] * NSL
        p_free = [None, None]
        pg_copied = {}
        e_read = [None, None]
        pg_read = [[], []]
        hw_read = [None, None]
        ht_read = [None, None]
        row_free = [None, None]
        ch_free = [None, None]
        trf = [tr_free[0], tr_free[1]]
        qa_free = [None, None]
        aw_free = [None] * 4
        e2_read = [None, None]
        aw_sent = None
        aw_ready = {}
        state = {"tr": 0, "ch": 0, "t2": None, "x1": None, "gt": 0, "aw": None}

        def edge_rows(t):
            return 128 if t < T - 1 else LASTP

        def base_reg(e, ap, top=N - 128):
            return e.value_load(ap, min_val=0, max_val=top)

        def adjacency_tile(t):
            w, i = divmod(t, TA)
            sl = t % NSL
            b = bank[2 + w % 2]
            K = edge_rows(t)
            op("dve", lambda e: e.tensor_scalar(Mr[:, sl, :], iotN[:, 0:128], c1[:, t:t + 1], None, ALU.is_equal),
               code_done, m_read[sl])
            ev = op("dve", lambda e: e.tensor_scalar(Nr[:, sl, :], iotN[:, :], bcol[:, t:t + 1], None, ALU.is_equal))
            ev = op("pe", lambda e: e.matmul(b[:, 0:NB], Mr[0:K, sl, :], Nr[0:K, sl, :], start=(i == 0),
                                             stop=(w == 0 and i == TA - 1)),
                    ev, qa_free[w % 2] if i == 0 else None)
            m_read[sl] = ev
            if i == 0 and w > 0:
                state["e2"] = op("dve", lambda e: e.tensor_scalar(E2[:, w % 2, :], iot[:, :], pd2[:, w:w + 1], None, ALU.is_equal),
                                 pd_done, e2_read[w % 2])
            if i == TA - 1:
                if w > 0:
                    ev = op("pe", lambda e: e.matmul(b[:, 0:NB], E2[:, w % 2, :], Aw[:, (w - 1) % 4, :], start=False, stop=True),
                            state["e2"], aw_ready[w - 1])
                    e2_read[w % 2] = ev
                    aw_ready["read", w - 1] = ev
                ev = op("act", lambda e: e.copy(Aw[:, w % 4, :], b[:, 0:NB]), ev, aw_free[w % 4], aw_ready.get(("read", w - 4)))
                qa_free[w % 2] = ev
                aw_ready[w] = ev
                def send(e):
                    r = base_reg(e, ba2i[0:1, w:w + 1], 8 * (N - 16))
                    return e.dma_start(Adw[bass.ds(r, 128), :], Aw[:, w % 4, :])
                state["aw"] = dma("sp", send, "aw", ev, state["aw"], base_done)
                aw_free[w % 4] = state["aw"]

        def transpose_window(src_ap, ready, copy_func):
            n = state["tr"]
            state["tr"] += 1
            b = bank[6 + n % 2]
            Q.wait("pe", ready, trf[n % 2])
            for k in range(2):
                ev = op("pe", lambda e, k=k: e.transpose(b[:, k * 128:(k + 1) * 128], src_ap[:, k * 128:(k + 1) * 128], idn[:, :]),
                        sig=(k == 1))
            return b, ev, n

        def after_first(g):
            s = g % 2
            box = {}

            def a():
                box["h"] = op("dve", lambda e: e.tensor_tensor(hw[:, s, :], Pg[:, s, :], b1[:, :], ALU.add),
                              pg_copied[g], hw_read[s], ldw)
                pg_read[s].append(box["h"])

            def b_():
                b, ev, n = transpose_window(hw[:, s, :], box["h"], None)
                hw_read[s] = ev
                ev = op("act", lambda e: e.activation(hTw[:, s, :], b[:, 0:256], ACT.Relu), ev, ht_read[s])
                trf[n % 2] = ev
                box["hT"] = ev

            def chunk(c):
                def f():
                    n = state["ch"]
                    state["ch"] += 1
                    b = bank[4 + n % 2]
                    Q.wait("pe", box["hT"], W2_done, ch_free[n % 2])
                    for k in range(2):
                        ev = op("pe", lambda e, k=k: e.matmul(b[:, :], hTw[:, s, k * 128:(k + 1) * 128],
                                                              W2[:, k, c * 512:(c + 1) * 512], start=(k == 0), stop=(k == 1)),
                                sig=(k == 1))
                    ht_read[s] = ev
                    ev = op("act", lambda e: e.copy(rowb[:, s, c * 512:(c + 1) * 512], b[:, :]), ev, row_free[s])
                    ch_free[n % 2] = ev
                    if c == 3:
                        def send(e):
                            r = base_reg(e, bai[0:1, g:g + 1])
                            return e.dma_start(T2[bass.ds(r, 128), :], rowb[:, s, :])
                        state["t2"] = dma("sp", send, "t2a", ev, state["t2"])
                        row_free[s] = state["t2"]
                return f
            return [a, b_] + [chunk(c) for c in range(4)]

        def layernorm(y, o, rows, s, ready, *free):
            ev = op("dve", lambda e: e.bn_stats(st[0:rows, s, :], y), ready)
            ev = op("dve", lambda e: e.bn_aggr(sm[0:rows, s, 0:2], st[0:rows, s, :]), ev)
            ev = op("act", lambda e: e.activation(sm[0:rows, s, 2:3], sm[0:rows, s, 1:2], ACT.Sqrt, bias=eps[0:rows, 0:1]), ev)
            ev = op("dve", lambda e: e.reciprocal(sm[0:rows, s, 3:4], sm[0:rows, s, 2:3]), ev)
            return op("dve", lambda e: e.tensor_scalar(o, y, sm[0:rows, s, 0:1], sm[0:rows, s, 3:4], ALU.subtract, ALU.mult), ev, *free)

        x1_free = [None, None]
        xw_in = {}

        def load_xw(g):
            def send(e):
                r = base_reg(e, bai[0:1, g:g + 1])
                return e.dma_start(xw[:, g % 2, :], x[bass.ds(r, 128), :])
            xw_in[g] = dma("sp", send, f"xw{g % 2}", *xw_read[g % 2])

        xw_read = [[], []]

        def after_second(g):
            s = g % 2

            def a():
                ev = op("dve", lambda e: e.tensor_tensor(hw[:, s, :], Pg[:, s, :], b2[:, :], ALU.add),
                        pg_copied[g], hw_read[s], ldw)
                pg_read[s].append(ev)
                ev = op("dve", lambda e: e.tensor_tensor(hw[:, s, :], hw[:, s, :], xw[:, s, :], ALU.add), ev, xw_in[g])
                xw_read[s][:] = [ev]
                ev = layernorm(hw[:, s, :], x1w[:, s, :], 128, s, ev, x1_free[s])

                def send(e):
                    r = base_reg(e, bai[0:1, g:g + 1])
                    return e.dma_start(X1[bass.ds(r, 128), :], x1w[:, s, :])
                state["x1"] = dma("sp", send, "x1", ev, state["x1"])
                x1_free[s] = state["x1"]
                if g + 2 < NW:
                    load_xw(g + 2)
            return [a]

        def relational(layer, table, table_done, extra):
            todo = {}
            Q.wait("pool", *table_done)
            for t in range(T):
                g, i = divmod(t, TW)
                n = state["gt"]
                state["gt"] += 1
                sl, ss = n % NG, n % NSL
                K = edge_rows(t)
                last = i == TW - 1 or t == T - 1
                ge = dma("pool", lambda e, sl=sl, t=t, K=K: e.indirect_dma_start(
                    G[0:K, sl, :], None, table, bass.IndirectOffsetOnAxis(ap=idx[0:K, t:t + 1], axis=0)),
                    f"g{sl}", g_read[sl], idx_done)
                se = op("dve", lambda e, ss=ss, t=t: e.tensor_scalar(S[:, ss, :], iot[:, :], dl[:, t:t + 1], wgt[:, t:t + 1],
                                                                     ALU.is_equal, ALU.mult), dl_done, s_read[ss])
                ev = op("pe", lambda e, g=g, sl=sl, ss=ss, i=i, K=K, last=last: e.matmul(
                    bank[g % 2][:, 0:256], S[0:K, ss, :], G[0:K, sl, :], start=(i == 0), stop=(g == 0 and last)),
                    ge, se, p_free[g % 2] if i == 0 else None)
                g_read[sl] = s_read[ss] = ev
                if i == 2 and g > 0:
                    state["e1"] = op("dve", lambda e, g=g: e.tensor_scalar(Ew[:, g % 2, :], iot[:, :], pd1[:, g:g + 1], None,
                                                                           ALU.is_equal), pd_done, e_read[g % 2])
                if last:
                    if g > 0:
                        ev = op("pe", lambda e, g=g: e.matmul(bank[g % 2][:, 0:256], Ew[:, g % 2, :], Pg[:, (g - 1) % 2, :],
                                                              start=False, stop=True), state["e1"], pg_copied[g - 1])
                        e_read[g % 2] = ev
                        pg_read[(g - 1) % 2].append(ev)
                    pr = list(pg_read[g % 2])
                    pg_read[g % 2] = []
                    ev = op("act", lambda e, g=g: e.copy(Pg[:, g % 2, :], bank[g % 2][:, 0:256]), ev, *pr)
                    p_free[g % 2] = ev
                    pg_copied[g] = ev
                    steps = after_first(g) if layer == 0 else after_second(g)
                    for k, f in enumerate(steps):
                        todo.setdefault(t + 2 + 3 * k, []).append(f)
                for f in todo.pop(t, []):
                    f()
                extra(t)
            for t in sorted(todo):
                for f in todo[t]:
                    f()

        relational(0, T1g, table1_done, adjacency_tile)

        def adjacency_block(t):
            if t < JB:
                state["A"] = dma("act", lambda e: e.dma_start(A_sb[0:PB, t, :], Ad[t * PB:(t + 1) * PB, 0:N]), "ar0",
                                 state["aw"], state["t2"], W2_done)

        load_xw(0)
        load_xw(1)
        relational(1, T2g, [state["t2"]], adjacency_block)

        handover = [("pe", Q.n["pe"]), ("act", Q.n["act"]), ("dve", Q.n["dve"]), state["x1"]]
        A_done = state["A"]

        rd = []
        bfree = [None] * 8
        for i in range(4):
            bfree[i] = None
        for c in range(NC):
            b = c % 2
            Q.wait("pe", A_done, bfree[b], *handover)
            for j in range(JB):
                ev = op("pe", lambda e, b=b, j=j, c=c: e.matmul(bank[b][:, 0:CH], ones[0:PB, :], A_sb[0:PB, j, c * CH:(c + 1) * CH],
                                                                start=(j == 0), stop=(j == JB - 1)), sig=(j == JB - 1))
            ev = op("dve", lambda e, b=b, c=c: e.tensor_scalar(rdeg[:, c * CH:(c + 1) * CH], bank[b][:, 0:CH], 1.0, None, ALU.max),
                    ev, *handover)
            bfree[b] = ev
            ev = op("dve", lambda e, c=c: e.reciprocal(rdeg[:, c * CH:(c + 1) * CH], rdeg[:, c * CH:(c + 1) * CH]), ev)
            rd.append(ev)

        X1s = X1.rearrange("(j p) f -> p j f", p=PB)
        hs_read = None
        hs_done = [None] * JB
        hT_done = [None] * NC
        xs_t = [agT[0:PB, s, :, :].rearrange("p k c -> p (k c)").rearrange("p (j f) -> p j f", f=250) for s in range(2)]

        x1b = [view(RB, 30720 + 20000 + 8000 + 10016 + 1024 * s, (256,), F32) for s in range(2)]
        x1r = [None, None]

        def load_x1(j, sem):
            s = j % 2
            return dma("sp", lambda e: e.dma_start(x1b[s][0:PB, :], X1[j * PB:(j + 1) * PB, :]), f"{sem}{s}",
                       x1r[s], state["x1"], *handover)

        def split(j, ev, b):
            t_ = tmp[j % 2]
            Q.wait("act", hs_free)
            e0 = op("act", lambda e: e.copy(hs[0:PB, j, 0, :], b[0:PB, 0:256]), ev)
            e1 = op("dve", lambda e: e.tensor_tensor(t_[0:PB, :], b[0:PB, 0:256], hs[0:PB, j, 0, :], ALU.subtract), e0, tmp_read[j % 2])
            e2 = op("act", lambda e: e.copy(hs[0:PB, j, 1, :], t_[0:PB, :]), e1)
            e3 = op("dve", lambda e: e.tensor_tensor(hs[0:PB, j, 2, :], t_[0:PB, :], hs[0:PB, j, 1, :], ALU.subtract), e2)
            tmp_read[j % 2] = e3
            hs_done[j] = e3
            return e1

        tmp = [sb(f"tmp{i}", [128, 256], F32) for i in range(2)]
        tmp_read = [None, None]
        hs_free = None

        lx = {0: load_x1(0, "xs"), 1: load_x1(1, "xs")}
        at_read = [None, None]
        for c in range(NC):
            s = c % 2
            evs = []
            for jj in range(4):
                j = 4 * c + jj
                n = state["tr"]
                state["tr"] += 1
                b = bank[6 + n % 2]
                Q.wait("pe", lx[j], trf[n % 2])
                for k in range(2):
                    ev = op("pe", lambda e, b=b, j=j, k=k: e.transpose(b[:, k * 128:k * 128 + PB], x1b[j % 2][0:PB, k * 128:(k + 1) * 128],
                                                                       idn[0:PB, 0:PB]), sig=(k == 1))
                x1r[j % 2] = ev
                if j + 2 < JB:
                    lx[j + 2] = load_x1(j + 2, "xs")
                i_ = b[:, 0:256].rearrange("p (k n) -> p k n", n=128)[:, :, 0:PB]
                ev = op("act", lambda e, s=s, jj=jj, i_=i_: e.copy(agT[:, s, :, jj * PB:(jj + 1) * PB], i_), ev, at_read[s], *handover)
                trf[n % 2] = ev
                evs.append(ev)
            for m in range(2):
                b = 4 + m
                Q.wait("pe", bfree[b], *evs)
                for k in range(2):
                    ev = op("pe", lambda e, b=b, m=m, k=k, s=s: e.matmul(bank[b][:, 0:CH], wts[:, 0, k, m * 128:(m + 1) * 128],
                                                                         agT[:, s, k, :], start=(k == 0), stop=(k == 1)), sig=(k == 1))
                at_read[s] = ev
                ev = op("act", lambda e, b=b, m=m, c=c: e.activation(hT[:, m, c * CH:(c + 1) * CH], bank[b][:, 0:CH], ACT.Identity,
                                                                     bias=bT[:, m:m + 1]), ev)
                bfree[b] = ev
                hT_done[c] = ev

        def node_major(j):
            n = state["tr"]
            state["tr"] += 1
            b = bank[6 + n % 2]
            Q.wait("pe", hT_done[j // 4], trf[n % 2])
            for k in range(2):
                ev = op("pe", lambda e, k=k: e.transpose(b[0:PB, k * 128:(k + 1) * 128], hT[:, k, j * PB:(j + 1) * PB], idn[:, :]),
                        sig=(k == 1))
            trf[n % 2] = split(j, ev, b)

        for l in range(3):
            for j in range(JB):
                node_major(j)
            hT_next = [None] * NC
            for c in range(NC):
                s = c % 2
                for m in range(2):
                    b = m
                    Q.wait("pe", bfree[b])
                    for j in range(JB):
                        Q.wait("pe", hs_done[j])
                        for q in range(3):
                            end = j == JB - 1 and q == 2
                            ev = op("pe", lambda e, b=b, j=j, q=q, m=m, c=c, end=end: e.matmul(
                                bank[b][:, 0:CH], hs[0:PB, j, q, m * 128:(m + 1) * 128], A_sb[0:PB, j, c * CH:(c + 1) * CH],
                                start=(j == 0 and q == 0), stop=end), sig=end)
                    hs_free = ev
                    ev = op("dve", lambda e, b=b, s=s, m=m, c=c: e.tensor_tensor(agT[:, s, m, :], bank[b][:, 0:CH],
                                                                                 rdeg[:, c * CH:(c + 1) * CH], ALU.mult),
                            ev, rd[c], at_read[s])
                    bfree[b] = ev
                evs = []
                for m in range(2):
                    b = 4 + m
                    Q.wait("pe", bfree[b], ev, hT_done[c])
                    for k in range(4):
                        w_ = wts[:, 1 + 2 * l + k // 2, k % 2, m * 128:(m + 1) * 128]
                        r_ = agT[:, s, k % 2, :] if k < 2 else hT[:, k % 2, c * CH:(c + 1) * CH]
                        pe_ = op("pe", lambda e, b=b, w_=w_, r_=r_, k=k: e.matmul(bank[b][:, 0:CH], w_, r_, start=(k == 0), stop=(k == 3)),
                                 sig=(k == 3))
                at_read[s] = pe_
                for m in range(2):
                    b = 4 + m
                    ev = op("act", lambda e, b=b, m=m, c=c, l=l: e.activation(hT[:, m, c * CH:(c + 1) * CH], bank[b][:, 0:CH], ACT.Relu,
                                                                              bias=bT[:, 2 + 2 * l + m:3 + 2 * l + m]), pe_)
                    bfree[b] = ev
                    hT_next[c] = ev
            hT_done = hT_next

        lx = {0: load_x1(0, "xs"), 1: load_x1(1, "xs")}
        o_free = [None, None]
        yb = [agT[0:PB, s, 0, 0:256] for s in range(2)]
        ob = [agT[0:PB, s, 1, 0:256] for s in range(2)]
        for j in range(JB):
            s = j % 2
            Q.wait("pe", hT_done[j // 4], bfree[s])
            for k in range(2):
                ev = op("pe", lambda e, s=s, j=j, k=k: e.matmul(bank[s][0:PB, 0:256], hT[:, k, j * PB:(j + 1) * PB], wts[:, 7, k, :],
                                                                start=(k == 0), stop=(k == 1)), sig=(k == 1))
            ev = op("dve", lambda e, s=s: e.tensor_tensor(yb[s], bank[s][0:PB, 0:256], bo[0:PB, :], ALU.add), ev, at_read[0], at_read[1])
            bfree[s] = ev
            ev = op("dve", lambda e, s=s: e.tensor_tensor(yb[s], yb[s], x1b[s][0:PB, :], ALU.add), ev, lx[j])
            x1r[s] = ev
            if j + 2 < JB:
                lx[j + 2] = load_x1(j + 2, "xs")
            ev = layernorm(yb[s], ob[s], PB, s, ev, o_free[s])
            o_free[s] = dma("sp", lambda e, s=s, j=j: e.dma_start(out[j * PB:(j + 1) * PB, :], ob[s]), f"o{s}", ev)
        Q.wait("sp", *o_free)

        block = ctx.enter_context(nc.Block())

        def run(eng, e):
            for f in Q.ops[eng][:head[eng]]:
                f(e)
            e.wait_ge(sems["dve"], flag_done[1])
            fast = e.value_load(flag[0:1, 0:1], min_val=0, max_val=1)
            with e.If(fast):
                for f in Q.ops[eng][head[eng]:]:
                    f(e)
            with e.Else():
                if eng == "dve":
                    for name, n in all_done:
                        e.wait_ge(sems[name], n)
                    e.sem_inc(sems["k_" + relay.first(relay.top[0])], 1)
                relay.emit(eng, e, relay.top, None, {})

        @block.tensor
        def _(e):
            run("pe", e)

        @block.scalar
        def _(e):
            run("act", e)

        @block.vector
        def _(e):
            run("dve", e)

        @block.gpsimd
        def _(e):
            run("pool", e)

        @block.sync
        def _(e):
            run("sp", e)


def kernel(x, src, dst, edge_type_8, edge_weight1, L0_gnn_basis, L0_gnn_coeff, L0_gnn_bias, L1_gnn_W_in, L1_gnn_b_in,
           L1_gnn_W_agg, L1_gnn_W_self, L1_gnn_b_hid, L1_gnn_W_out, L1_gnn_b_out):
    import numpy as np
    import concourse.bacc as bacc
    from concourse import mybir as mb
    from concourse.bass_utils import run_bass_kernel_spmd as run

    def tiles(a, pad):
        a = np.asarray(a).reshape(-1)
        a = np.concatenate([a, np.full(T * 128 - E, pad, a.dtype)])
        return np.ascontiguousarray(a.reshape(T, 128).T)

    dst = np.asarray(dst)
    arrays = {
        "x": np.asarray(x),
        "srcT": tiles(src, 0),
        "dstT": tiles(dst, N - 1),
        "etT": tiles(edge_type_8, 0),
        "wT": tiles(edge_weight1, 0.0),
        "first": np.ascontiguousarray(dst[::TW * 128].reshape(1, NW)),
        "first2": np.ascontiguousarray(dst[::TA * 128].reshape(1, NA)),
        "basis": np.asarray(L0_gnn_basis),
        "coeff": np.asarray(L0_gnn_coeff).reshape(1, 128),
        "bias": np.asarray(L0_gnn_bias),
        "W_in": np.asarray(L1_gnn_W_in),
        "b_cols": np.ascontiguousarray(np.concatenate([np.asarray(L1_gnn_b_in).reshape(2, 128),
                                                       np.asarray(L1_gnn_b_hid).reshape(6, 128)]).T),
        "b_rows": np.concatenate([np.asarray(L1_gnn_b_in).reshape(1, D), np.asarray(L1_gnn_b_hid)]).reshape(1, 4 * D),
        "W_agg": np.asarray(L1_gnn_W_agg),
        "W_self": np.asarray(L1_gnn_W_self),
        "W_out": np.asarray(L1_gnn_W_out),
        "b_out": np.asarray(L1_gnn_b_out).reshape(1, D),
    }
    arrays = {k: np.ascontiguousarray(v) for k, v in arrays.items()}
    nc = bacc.Bacc("TRN2", target_bir_lowering=False, num_devices=1)
    h = {k: nc.dram_tensor("in_" + k, v.shape, mb.dt.from_np(v.dtype), kind="ExternalInput").ap() for k, v in arrays.items()}
    o = nc.dram_tensor("out", (N, D), mb.dt.float32, kind="ExternalOutput").ap()
    program(nc, h["x"], h["srcT"], h["dstT"], h["etT"], h["wT"], h["first"], h["first2"], h["basis"], h["coeff"], h["bias"],
            h["W_in"], h["b_cols"], h["W_agg"], h["W_self"], h["b_rows"], h["W_out"], h["b_out"], o)
    r = run(nc, [{"in_" + k: v for k, v in arrays.items()}], core_ids=[0])
    return r.results[0]["out"]
```

```python
from contextlib import ExitStack

import concourse.bass as bass
from concourse import mybir

F32 = mybir.dt.float32
BF16 = mybir.dt.bfloat16
F32R = mybir.dt.float32r
U8 = mybir.dt.uint8
F16 = mybir.dt.float16
I32 = mybir.dt.int32
ALU = mybir.AluOpType
ACT = mybir.ActivationFunctionType
AX = mybir.AxisListType.X
RMAX = bass.bass_isa.ReduceOp.max

N = 2500
D = 256
E = 82500
R = 8
T = 645
LASTP = E - (T - 1) * 128
TA = 3
NA = 215
SW = 10
TW = SW * TA
NW = 22
ZC = 144
NB = 320
NS = 8 * NB
JB = 20
PB = 125
CH = 500
NC = 5
NG = 16
NSL = 8
AHEAD = 6
NR = 8
DG = 100
EPS = 1e-5


class Queues:

    def __init__(self, sems):
        self.ops = {e: [] for e in ("pe", "act", "dve", "pool", "sp")}
        self.sems = sems
        self.n = {}
        self.seen = {}

    def wait(self, eng, *events):
        for ev in events:
            if ev is None:
                continue
            sem, v = ev
            if self.seen.get((eng, sem), 0) < v:
                self.seen[(eng, sem)] = v
                self.ops[eng].append(lambda e, s=self.sems[sem], v=v: e.wait_ge(s, v))

    def op(self, eng, fn, *events, sig=True):
        self.wait(eng, *events)
        if not sig:
            self.ops[eng].append(fn)
            return None
        s = self.sems[eng]
        self.ops[eng].append(lambda e: fn(e).then_inc(s, 1))
        self.n[eng] = self.n.get(eng, 0) + 1
        return eng, self.n[eng]

    def dma(self, eng, fn, sem, *events):
        self.wait(eng, *events)
        s = self.sems[sem]
        self.ops[eng].append(lambda e: fn(e).then_inc(s, 16))
        self.n[sem] = self.n.get(sem, 0) + 16
        return sem, self.n[sem]


class Names:
    pass


class Relay:

    def __init__(self, sems):
        self.sems = sems
        self.top = []
        self.at = [self.top]

    def step(self, eng, fn):
        self.at[-1].append((eng, fn))

    def loop(self, name, count, fill):
        body = []
        self.at[-1].append((None, name, count, body))
        self.at.append(body)
        fill()
        self.at.pop()

    def first(self, item):
        return item[0] or self.first(item[3][0])

    def engines(self, body):
        got = set()
        for item in body:
            got |= {item[0]} if item[0] else self.engines(item[3])
        return got

    def emit(self, eng, e, body, after, v):
        for n, item in enumerate(body):
            nxt = self.first(body[n + 1]) if n + 1 < len(body) else after
            if item[0] is None:
                _, name, count, inner = item
                assert nxt in (None, self.first(inner[0]))
                if eng in self.engines(inner):
                    with e.Fori(0, count) as i:
                        self.emit(eng, e, inner, self.first(inner[0]), {**v, name: i})
            elif item[0] == eng:
                own = self.sems["k_" + eng]
                e.wait_ge(own, 1)
                e.sem_clear(own)
                give = self.sems["k_" + (nxt or "end")]
                if eng == "sp":
                    item[1](e, v).then_inc(self.sems["k_dma"], 16)
                    e.wait_ge(self.sems["k_dma"], 16)
                    e.sem_clear(self.sems["k_dma"])
                    e.sem_inc(give, 1)
                elif eng == "pool":
                    item[1](e, v).then_inc(self.sems["k_gather"], 16)
                    e.drain().then_inc(give, 1)
                else:
                    item[1](e, v).then_inc(give, 1)


def general(relay, m):
    dve, act, pe, sp, pool = (lambda fn, g=g: relay.step(g, fn) for g in ("dve", "act", "pe", "sp", "pool"))

    def rows(ap, v):
        return ap[bass.ds(v["k"] * PB, PB), :]

    def sums(table, index, key, weight):
        dve(lambda e, v: e.memset(m.acc, 0.0))

        def tile():
            dve(lambda e, v: e.tensor_copy(m.ix, index[:, bass.ds(v["t"], 1)]))
            dve(lambda e, v: e.tensor_copy(m.dw[:, 0:1], key[:, bass.ds(v["t"], 1)]))
            dve(lambda e, v: e.tensor_copy(m.dw[:, 1:2], weight[:, bass.ds(v["t"], 1)]))
            dve(lambda e, v: e.tensor_tensor(m.dw[:, 0:1], m.dw[:, 0:1], m.base, ALU.subtract))
            dve(lambda e, v: e.tensor_scalar(m.S, m.iot, m.dw[:, 0:1], m.dw[:, 1:2], ALU.is_equal, ALU.mult))
            pool(lambda e, v: e.indirect_dma_start(m.G, None, table, bass.IndirectOffsetOnAxis(ap=m.ix, axis=0)))
            pe(lambda e, v: e.matmul(m.bank[0][:, 0:256], m.S, m.G, start=True, stop=True))
            pe(lambda e, v: e.matmul(m.bank[1][:, 0:1], m.S, m.onef, start=True, stop=True))
            dve(lambda e, v: e.tensor_tensor(m.acc[:, 0:256], m.acc[:, 0:256], m.bank[0][:, 0:256], ALU.add))
            dve(lambda e, v: e.tensor_tensor(m.acc[:, 256:257], m.acc[:, 256:257], m.bank[1][:, 0:1], ALU.add))

        relay.loop("t", T, tile)

    def turned(src, dst):
        for k in range(2):
            pe(lambda e, v, k=k: e.transpose(m.bank[2][:, k * 128:k * 128 + PB], src[0:PB, k * 128:(k + 1) * 128], m.idn[0:PB, 0:PB]))
        act(lambda e, v: e.copy(dst[:, :, 0:PB], m.bank[2][:, 0:256].rearrange("p (k n) -> p k n", n=128)[:, :, 0:PB]))

    def product(pairs, cols=256):
        n = 2 * len(pairs)
        for i, (hT_, w_) in enumerate(pairs):
            for k in range(2):
                pe(lambda e, v, hT_=hT_, w_=w_, k=k, i=i: e.matmul(m.bank[3][0:PB, 0:cols], hT_[:, k, 0:PB], w_[:, k, :],
                                                                   start=(i == 0 and k == 0), stop=(2 * i + k == n - 1)))

    def norm(y, o):
        dve(lambda e, v: e.bn_stats(m.st[0:PB, 0, :], y[0:PB, :]))
        dve(lambda e, v: e.bn_aggr(m.sm[0:PB, 0, 0:2], m.st[0:PB, 0, :]))
        act(lambda e, v: e.activation(m.sm[0:PB, 0, 2:3], m.sm[0:PB, 0, 1:2], ACT.Sqrt, bias=m.eps[0:PB, 0:1]))
        dve(lambda e, v: e.reciprocal(m.sm[0:PB, 0, 3:4], m.sm[0:PB, 0, 2:3]))
        dve(lambda e, v: e.tensor_scalar(o[0:PB, :], y[0:PB, :], m.sm[0:PB, 0, 0:1], m.sm[0:PB, 0, 3:4], ALU.subtract, ALU.mult))

    def blocks(fill):
        dve(lambda e, v: e.memset(m.base, 0.0))

        def body():
            fill()
            dve(lambda e, v: e.tensor_scalar(m.base, m.base, float(PB), None, ALU.add))
        relay.loop("k", JB, body)

    def table():
        dve(lambda e, v: e.memset(m.z, 0.0))
        sp(lambda e, v: e.dma_start(m.z[0:PB, :], rows(m.x, v)))
        turned(m.z, m.hT)
        row(m.W1)
        sp(lambda e, v: e.dma_start(rows(m.T1, v), m.row[0:PB, :]))

    def row(W):
        for c in range(4):
            product([(m.hT, W[:, :, c * 512:(c + 1) * 512])], 512)
            act(lambda e, v, c=c: e.copy(m.row[0:PB, c * 512:(c + 1) * 512], m.bank[3][0:PB, :]))

    def first():
        sums(m.T1g, m.idx, m.df, m.wgt)
        dve(lambda e, v: e.tensor_tensor(m.y, m.acc[:, 0:256], m.b1, ALU.add))
        dve(lambda e, v: e.tensor_scalar(m.y, m.y, 0.0, None, ALU.max))
        turned(m.y, m.hT)
        row(m.W2)
        sp(lambda e, v: e.dma_start(rows(m.T2, v), m.row[0:PB, :]))

    def second():
        sums(m.T2g, m.idx, m.df, m.wgt)
        dve(lambda e, v: e.tensor_tensor(m.y, m.acc[:, 0:256], m.b2, ALU.add))
        sp(lambda e, v: e.dma_start(m.z[0:PB, :], rows(m.x, v)))
        dve(lambda e, v: e.tensor_tensor(m.y[0:PB, :], m.y[0:PB, :], m.z[0:PB, :], ALU.add))
        norm(m.y, m.z)
        sp(lambda e, v: e.dma_start(rows(m.X1, v), m.z[0:PB, :]))
        turned(m.z, m.hT)
        product([(m.hT, m.wts[:, 0, :, :])])
        dve(lambda e, v: e.tensor_tensor(m.y[0:PB, :], m.bank[3][0:PB, 0:256], m.brow4[0:PB, 0, :], ALU.add))
        sp(lambda e, v: e.dma_start(rows(m.H[0], v), m.y[0:PB, :]))

    def sage(l):
        def f():
            sums(m.H[l], m.di, m.sf, m.wone)
            dve(lambda e, v: e.tensor_scalar(m.acc[:, 256:257], m.acc[:, 256:257], 1.0, None, ALU.max))
            sp(lambda e, v: e.dma_start(m.z[0:PB, :], rows(m.H[l], v)))
            dve(lambda e, v: e.reciprocal(m.acc[:, 256:257], m.acc[:, 256:257]))
            dve(lambda e, v: e.tensor_scalar(m.y, m.acc[:, 0:256], m.acc[:, 256:257], None, ALU.mult))
            turned(m.y, m.hT)
            turned(m.z, m.hT2)
            product([(m.hT, m.wts[:, 1 + 2 * l, :, :]), (m.hT2, m.wts[:, 2 + 2 * l, :, :])])
            dve(lambda e, v: e.tensor_tensor(m.y[0:PB, :], m.bank[3][0:PB, 0:256], m.brow4[0:PB, 1 + l, :], ALU.add))
            dve(lambda e, v: e.tensor_scalar(m.y, m.y, 0.0, None, ALU.max))
            sp(lambda e, v: e.dma_start(rows(m.H[l + 1], v), m.y[0:PB, :]))
        return f

    def last():
        sp(lambda e, v: e.dma_start(m.z[0:PB, :], rows(m.H[3], v)))
        turned(m.z, m.hT)
        product([(m.hT, m.wts[:, 7, :, :])])
        sp(lambda e, v: e.dma_start(m.z[0:PB, :], rows(m.X1, v)))
        dve(lambda e, v: e.tensor_tensor(m.y[0:PB, :], m.bank[3][0:PB, 0:256], m.bo[0:PB, :], ALU.add))
        dve(lambda e, v: e.tensor_tensor(m.y[0:PB, :], m.y[0:PB, :], m.z[0:PB, :], ALU.add))
        norm(m.y, m.z)
        sp(lambda e, v: e.dma_start(rows(m.out, v), m.z[0:PB, :]))

    dve(lambda e, v: e.memset(m.onef, 1.0))
    dve(lambda e, v: e.tensor_copy(m.df, m.di))
    dve(lambda e, v: e.tensor_copy(m.sf, m.si))
    dve(lambda e, v: e.tensor_scalar(m.t_, m.sf, 8.0, None, ALU.mult))
    dve(lambda e, v: e.tensor_copy(m.wone, m.ei))
    dve(lambda e, v: e.tensor_tensor(m.t_, m.t_, m.wone, ALU.add))
    dve(lambda e, v: e.tensor_copy(m.idx, m.t_))
    for l, W in ((0, m.W1), (1, m.W2)):
        for r in range(R):
            for b in range(R):
                o = W[:, :, r * 256:(r + 1) * 256]
                c = m.cf[:, l * 64 + r * 8 + b:l * 64 + r * 8 + b + 1]
                i_ = m.bas[l][:, b, :, :]
                if b == 0:
                    dve(lambda e, v, o=o, c=c, i_=i_: e.tensor_scalar(o, i_, c, None, ALU.mult))
                else:
                    dve(lambda e, v, o=o, c=c, i_=i_: e.scalar_tensor_tensor(o, i_, c, o, ALU.mult, ALU.add))
    sp(lambda e, v: e.dma_start(m.brow, m.b_rows.to_broadcast([128, 4 * D])))
    dve(lambda e, v: e.memset(m.wone, 1.0))
    dve(lambda e, v: e.tensor_scalar(m.wone[:, T - 1:T], m.ip, float(LASTP), None, ALU.is_lt))
    for f in (table, first, second, sage(0), sage(1), sage(2)):
        blocks(f)
    dve(lambda e, v: e.memset(m.base, 0.0))

    def body():
        dve(lambda e, v: e.memset(m.base, 0.0))
        last()
    relay.loop("k", JB, body)
    dve(lambda e, v: e.memset(m.base, 0.0))


def program(nc, x, srcT, dstT, etT, wT, large, small, basis, coeff, bias, W_in, b_in, W_agg, W_self,
            b_rows, W_out, b_out, out):
    def dram(name, shape, dt=F32):
        return nc.dram_tensor(name, shape, dt, kind="Internal").ap()

    H1 = dram("H1", (N, D))
    X1 = dram("X1", (N, D))
    Ad = dram("Ad", (N, NS), U8)
    T1, T2 = dram("T1", (N, R * D)), dram("T2", (N, R * D))
    H = [dram(f"H{i}_", (N, D)) for i in range(4)]

    with ExitStack() as ctx:
        def sb(n, s, d):
            return ctx.enter_context(nc.sbuf_tensor(n, s, d))

        names = (["pe", "act", "dve", "pool"] + [f"g{i}" for i in range(NG)]
                 + ["edge", "base", "wts", "bas0", "bas1", "aw", "h1", "x1", "xw0", "xw1", "ar", "k_pe", "k_act", "k_dve",
                    "k_pool", "k_sp", "k_end", "k_dma", "k_gather"] + [f"xs{i}" for i in range(4)] + [f"o{i}" for i in range(4)])
        sems = {n: ctx.enter_context(nc.semaphore("s_" + n)) for n in names}
        Q = Queues(sems)
        op, dma = Q.op, Q.dma
        size = {F32: 4, I32: 4, BF16: 2, F16: 2, U8: 1}

        def lay(reg, *items):
            off, got = 0, []
            for shape, dt in items:
                n = 1
                for s in shape:
                    n *= s
                nb = (n * size[dt] + 31) // 32 * 32
                assert off + nb <= reg.shape[1] * 4, (shape, off + nb)
                v = reg[:, off // 4:(off + nb) // 4]
                v = (v if dt == F32 else v.bitcast(dt))[:, 0:n]
                if len(shape) == 2:
                    v = v.rearrange("p (a b) -> p a b", b=shape[1])
                elif len(shape) == 3:
                    v = v.rearrange("p (a b c) -> p a b c", b=shape[1], c=shape[2])
                got.append(v)
                off += nb
            return got

        wts = sb("wts", [128, 8, 2, 256], F32)
        idn = sb("idn", [128, 128], F32)
        onef = sb("onef", [128, 128], F32)
        iot = sb("iot", [128, 128], F32)
        iotN = sb("iotN", [128, NB], F16)
        ip = sb("ip", [128, 1], F32)
        eps = sb("eps", [128, 1], F32)
        zero = sb("zero", [128, 1], F32)
        b1 = sb("b1", [128, 256], F32)
        b2 = sb("b2", [128, 256], F32)
        bo = sb("bo", [128, 256], F32)
        bT = sb("bT", [128, 8], F32)
        cf = sb("cf", [128, 128], F32)
        c1 = sb("c1", [128, T], F32)
        bcol = sb("bcol", [128, T], F32)
        c2 = sb("c2", [128, T], F32)
        wgt = sb("wgt", [128, T], F32)
        di = sb("di", [128, T], I32)
        si = sb("si", [128, T], I32)
        ei = sb("ei", [128, T], I32)
        ba = sb("ba", [128, NW], F32)
        bai = sb("bai", [128, NW], I32)
        pd1 = sb("pd1", [128, NW], F32)
        ba2 = sb("ba2", [128, NA], F32)
        ba2i = sb("ba2i", [128, NA], I32)
        pd2 = sb("pd2", [128, NA], F32)
        off = sb("off", [128, NA], I32)
        chk = sb("chk", [128, 16], F32)
        flag = sb("flag", [128, 1], I32)
        st = sb("st", [128, 4, 6], F32)
        sm = sb("sm", [128, 4, 4], F32)
        rdeg = sb("rdeg", [128, N], F32)
        hT = sb("hT", [128, 2, N], F32)
        RX = sb("RX", [128, 12800], F32)
        bas0, bas1, W1 = lay(RX, ((8, 2, 256), F32), ((8, 2, 256), F32), ((2, 2048), F32))
        bas = [bas0, bas1]
        A_sb = lay(RX, ((JB, N), U8))[0]
        df, sf, dl, aq = lay(hT[:, :, :].rearrange("p k n -> p (k n)"), *[((T,), F32)] * 4)
        with ExitStack() as inner:
            RY = inner.enter_context(nc.sbuf_tensor("RY", [128, 20480], F32))
        (W2, G, S, Zs, ZA, Pg, hw, h1w, xw, xT, Ew, Mr, Nr, Aw, Aw8, E2) = lay(
            RY, ((2, 2048), F32), ((NG, 256), F32), ((NSL, 128), F32), ((2, 256), F32), ((2, 16 * ZC), F32), ((2, 256), F32),
            ((2, 256), F32), ((2, 256), F32), ((2, 256), F32), ((2, 256), F32), ((2, 128), F32), ((NSL, 128), BF16),
            ((NSL, NB), BF16), ((4, NB), BF16), ((4, NB), U8), ((2, 128), BF16))
        ZA = ZA.rearrange("p s (q c) -> p s q c", c=ZC)
        hs = sb("hs", [128, JB, 2, 256], F32R)
        Ar = sb("Ar", [128, NR, CH], F32R)
        agT = sb("agT", [128, 2, 2, CH], F32)
        yb = sb("yb", [128, 4, 256], F32)
        ob = sb("ob", [128, 4, 256], F32)
        x1b = sb("x1b", [128, 4, 256], F32)

        bank = [ctx.enter_context(nc.psum_tensor(f"bank{i}", [128, 512], F32)) for i in range(8)]

        for t_, s_ in ((di, dstT), (ei, etT), (wgt, wT)):
            ld = dma("sp", lambda e, t_=t_, s_=s_: e.dma_start(t_[:, :], s_), "edge")
        dma("act", lambda e: e.dma_start(ba2i[:, :], small.to_broadcast([128, NA])), "base")
        dma("act", lambda e: e.dma_start(bai[:, :], large.to_broadcast([128, NW])), "base")
        ldb = dma("act", lambda e: e.dma_start(si[:, :], srcT), "base")
        dma("act", lambda e: e.dma_start(cf[:, :], coeff.to_broadcast([128, 128])), "bas0")
        ldbas = [dma("act", lambda e, l=l: e.dma_start(bas[l], basis[l].rearrange("b (k p) o -> p b k o", p=128)), f"bas{l}")
                 for l in range(2)]
        for i, w in enumerate([W_in, W_agg[0], W_self[0], W_agg[1], W_self[1], W_agg[2], W_self[2], W_out]):
            dma("sp", lambda e, i=i, w=w: e.dma_start(wts[:, i, :, :], w.rearrange("(k p) o -> p k o", p=128)), "wts")
        for t_, s_ in ((b1, bias[0:1, :]), (b2, bias[1:2, :]), (bo, b_out)):
            dma("sp", lambda e, t_=t_, s_=s_: e.dma_start(t_[:, :], s_.to_broadcast([128, 256])), "wts")
        ldw = dma("sp", lambda e: e.dma_start(bT[:, :], b_in), "wts")

        def iota(t_, n, step, mult):
            return op("pool", lambda e: e.iota(t_, pattern=[[step, n]], base=0, channel_multiplier=mult,
                                               allow_small_or_imprecise_dtypes=True))

        iota(ip[:, :], 1, 1, 1)
        iota(iot[:, :], 128, 1, 0)
        iot_done = iota(iotN[:, :], NB, 1, 0)

        def dve(fn, *ev):
            return op("dve", fn, *ev)

        dve(lambda e: e.memset(eps[:, :], EPS))
        zero_done = dve(lambda e: e.memset(zero[:, :], 0.0))
        idn_done = dve(lambda e: e.tensor_scalar(idn[:, :], iot[:, :], ip[:, 0:1], None, ALU.is_equal), iot_done)

        Q.wait("dve", ldb, ld)
        dve(lambda e: e.tensor_copy(ba[:, :], bai[:, :]))
        e1 = dve(lambda e: e.tensor_copy(ba2[:, :], ba2i[:, :]))
        df_done = dve(lambda e: e.tensor_copy(df, di[:, :]))
        dve(lambda e: e.tensor_scalar(ba[:, :], ba[:, :], float(N - 128), None, ALU.min), e1)
        ev = dve(lambda e: e.tensor_scalar(ba2[:, :], ba2[:, :], float(N - 16), None, ALU.min))
        dve(lambda e: e.memset(ba[:, 0:1], 0.0), ev)
        dve(lambda e: e.memset(ba[:, NW - 1:NW], float(N - 128)))
        dve(lambda e: e.memset(ba2[:, 0:1], 0.0))
        eb = dve(lambda e: e.memset(ba2[:, NA - 1:NA], float(N - 16)))
        nf = (NW - 1) * TW
        e1 = dve(lambda e: e.tensor_tensor(c1[:, :].rearrange("p (w t) -> p w t", t=TA), df.rearrange("p (w t) -> p w t", t=TA),
                                           ba2[:, :].unsqueeze(2).to_broadcast([128, NA, TA]), ALU.subtract), eb, df_done)
        dve(lambda e: e.tensor_tensor(dl[:, 0:nf].rearrange("p (w t) -> p w t", t=TW),
                                      df[:, 0:nf].rearrange("p (w t) -> p w t", t=TW),
                                      ba[:, 0:NW - 1].unsqueeze(2).to_broadcast([128, NW - 1, TW]), ALU.subtract))
        dve(lambda e: e.tensor_scalar(dl[:, nf:T], df[:, nf:T], ba[:, NW - 1:NW], None, ALU.subtract))
        dve(lambda e: e.tensor_tensor(pd1[:, 1:NW], ba[:, 1:NW], ba[:, 0:NW - 1], ALU.subtract))
        dve(lambda e: e.tensor_tensor(pd2[:, 1:NA], ba2[:, 1:NA], ba2[:, 0:NA - 1], ALU.subtract))
        ev = dve(lambda e: e.tensor_tensor(aq[:, 0:T - 2], df[:, 2:T], df[:, 0:T - 2], ALU.subtract))
        c2_done = dve(lambda e: e.scalar_tensor_tensor(c2[:, :], ei[:, :], 16.0, c1[:, :], ALU.mult, ALU.add), e1)
        low = [(dl, 0), (c1[:, :], 0), (pd1[:, 1:NW], 0), (pd2[:, 1:NA], 0), (aq[:, 0:T - 2], 1)]
        high = [(dl, 127), (c1[:, :], 15), (pd1[:, 1:NW], 128), (pd2[:, 1:NA], 16)]
        for n, (s_, _) in enumerate(low):
            ev = dve(lambda e, n=n, s_=s_: e.tensor_reduce(chk[:, n:n + 1], s_, AX, ALU.min), ev)
        for n, (s_, _) in enumerate(high):
            ev = dve(lambda e, n=n, s_=s_: e.tensor_reduce(chk[:, 5 + n:6 + n], s_, AX, ALU.max))
        for n, (_, v) in enumerate(low):
            ev = dve(lambda e, n=n, v=v: e.tensor_scalar(chk[:, n:n + 1], chk[:, n:n + 1], -1.0, float(v), ALU.mult, ALU.add), ev)
        for n, (_, v) in enumerate(high):
            ev = dve(lambda e, n=n, v=v: e.tensor_scalar(chk[:, 5 + n:6 + n], chk[:, 5 + n:6 + n], float(-v), None, ALU.add))
        ev = dve(lambda e: e.tensor_reduce(chk[:, 9:10], chk[:, 0:9], AX, ALU.max), ev)
        ev = op("pool", lambda e: e.partition_all_reduce(chk[:, 10:11], chk[:, 9:10], 128, RMAX), ev)
        flag_done = dve(lambda e: e.tensor_scalar(flag[:, :], chk[:, 10:11], 0.0, None, ALU.is_le), ev)

        all_done = [("pe", 0), ("act", 0), ("pool", Q.n["pool"]), ("dve", Q.n["dve"]), ldw, ld, ldb, *ldbas]
        head = {k: len(v) for k, v in Q.ops.items()}
        m = Names()
        m.T1g = T1.rearrange("n (r o) -> (n r) o", o=D)
        m.T2g = T2.rearrange("n (r o) -> (n r) o", o=D)
        m.T1, m.T2, m.X1, m.H, m.x, m.out, m.b_rows = T1, T2, X1, H, x, out, b_rows
        m.wgt, m.di, m.si, m.ei = wgt[:, :], di[:, :], si[:, :], ei[:, :]
        m.ip, m.iot, m.idn, m.b1, m.b2, m.bo, m.W1, m.wts = ip[:, :], iot[:, :], idn, b1[:, :], b2[:, :], bo, W1, wts
        m.st, m.sm, m.eps, m.bank, m.cf, m.bas = st, sm, eps, bank, cf, bas
        (m.W2, m.G, m.S, m.acc, m.y, m.z, m.hT, m.hT2, m.wone, m.brow, m.dw, m.onef, m.ix, m.base, m.row, m.df, m.sf, m.t_,
         m.idx) = lay(RY, ((2, 2048), F32), ((256,), F32), ((128,), F32), ((257,), F32), ((256,), F32), ((256,), F32),
                      ((2, 128), F32), ((2, 128), F32), ((T,), F32), ((4 * D,), F32), ((2,), F32), ((1,), F32), ((1,), I32),
                      ((1,), F32), ((2048,), F32), ((T,), F32), ((T,), F32), ((T,), F32), ((T,), I32))
        m.brow4 = m.brow.rearrange("p (l c) -> p l c", c=D)
        relay = Relay(sems)
        general(relay, m)

        e1 = dve(lambda e: e.tensor_copy(ba2i[:, :], ba2[:, :]))
        ev = dve(lambda e: e.tensor_copy(bai[:, :], ba[:, :]))
        base_done = ev
        ns = (NW - 1) * SW
        dve(lambda e: e.tensor_tensor(off[:, 0:ns].rearrange("p (w t) -> p w t", t=SW),
                                      ba2i[:, 0:ns].rearrange("p (w t) -> p w t", t=SW),
                                      bai[:, 0:NW - 1].unsqueeze(2).to_broadcast([128, NW - 1, SW]), ALU.subtract), ev)
        off_done = dve(lambda e: e.tensor_tensor(off[:, ns:NA], ba2i[:, ns:NA], bai[:, NW - 1:NW].to_broadcast([128, NA - ns]),
                                                 ALU.subtract))
        part_done = dve(lambda e: e.tensor_scalar(ba2i[:, :], ba2[:, :], 8.0, None, ALU.mult), off_done)
        dve(lambda e: e.tensor_scalar(pd1[:, 1:NW], pd1[:, 1:NW], -1.0, ip[:, 0:1], ALU.mult, ALU.add))
        pd_done = dve(lambda e: e.tensor_scalar(pd2[:, 1:NA], pd2[:, 1:NA], -8.0, ip[:, 0:1], ALU.mult, ALU.add))
        dve(lambda e: e.memset(onef[:, :], 1.0))

        chores = []
        marks = {}

        def relation_weights(l, W):
            for pair in range(4):
                last = [None, None]
                for b in range(8):
                    for q in range(2):
                        r = 2 * pair + q

                        def f(b=b, q=q, r=r, last=last):
                            o = W[:, :, r * 256:(r + 1) * 256]
                            c = cf[:, l * 64 + r * 8 + b:l * 64 + r * 8 + b + 1]
                            i_ = bas[l][:, b, :, :]
                            if b == 0:
                                last[q] = dve(lambda e: e.tensor_scalar(o, i_, c, None, ALU.mult), ldbas[l])
                            else:
                                last[q] = dve(lambda e: e.scalar_tensor_tensor(o, i_, c, o, ALU.mult, ALU.add), last[q])
                            marks["W", l] = last[q]
                        chores.append(f)

        def adjacency_codes():
            box = [None]

            def add(fn):
                def f():
                    box[0] = dve(fn, box[0])
                    marks["codes"] = box[0]
                chores.append(f)
            add(lambda e: e.tensor_copy(sf, si[:, :]))
            add(lambda e: e.tensor_scalar(aq, sf, float(NB), None, ALU.is_ge))
            for q in range(2, 8):
                add(lambda e, q=q: e.scalar_tensor_tensor(aq, sf, float(NB * q), aq, ALU.is_ge, ALU.add))
            add(lambda e: e.scalar_tensor_tensor(c1[:, :], c1[:, :], 8.0, aq, ALU.mult, ALU.add))
            add(lambda e: e.scalar_tensor_tensor(bcol[:, :], aq, float(-NB), sf, ALU.mult, ALU.add))

        relation_weights(0, W1)
        adjacency_codes()
        relation_weights(1, W2)

        Adw = Ad.rearrange("d (a b) -> (d a) b", b=NB)
        fr = {}
        z_at = {}
        pg_at, z_ready, aw_at = {}, {}, {}
        wrote = {"h1": None, "x1": None, "aw": None}

        def free(key):
            return fr.get(key, [])

        def edge_rows(t):
            return 128 if t < T - 1 else LASTP

        def base_reg(e, ap, top):
            return e.value_load(ap, min_val=0, max_val=top)

        hot_at, hot_n = {}, [0]

        def adjacency_tile(t):
            w, i = divmod(t, TA)
            sl = t % NSL
            b = bank[6 + w % 2]
            K = edge_rows(t)
            while hot_n[0] < min(T, t + 3):
                u = hot_n[0]
                hot_n[0] += 1
                us = u % NSL
                op("dve", lambda e, u=u, us=us: e.tensor_scalar(Mr[:, us, :], iotN[:, 0:128], c1[:, u:u + 1], None, ALU.is_equal),
                   marks["codes"], *free(("m", us)))
                hot_at[u] = op("dve", lambda e, u=u, us=us: e.tensor_scalar(Nr[:, us, :], iotN[:, :], bcol[:, u:u + 1], None,
                                                                            ALU.is_equal))
            ev = hot_at[t]
            ev = op("pe", lambda e: e.matmul(b[:, 0:NB], Mr[0:K, sl, :], Nr[0:K, sl, :], start=(i == 0),
                                             stop=(w == 0 and i == TA - 1)),
                    ev, *(free(("qa", w % 2)) if i == 0 else []))
            fr["m", sl] = [ev]
            if i == 0 and w > 0:
                marks["e2"] = op("dve", lambda e: e.tensor_scalar(E2[:, w % 2, :], iot[:, :], pd2[:, w:w + 1], None, ALU.is_equal),
                                 pd_done, *free(("e2", w % 2)))
            if i == TA - 1:
                if w > 0:
                    ev = op("pe", lambda e: e.matmul(b[:, 0:NB], E2[:, w % 2, :], Aw[:, (w - 1) % 4, :], start=False, stop=True),
                            marks["e2"], aw_at[w - 1])
                    fr["e2", w % 2] = [ev]
                    fr["aw", (w - 1) % 4] = [ev]
                op("act", lambda e: e.copy(Aw[:, w % 4, :], b[:, 0:NB]), ev, *free(("aw", w % 4)))
                aw_at[w] = ("act", Q.n["act"])
                ev = op("act", lambda e: e.copy(Aw8[:, w % 4, :], b[:, 0:NB]), *free(("aw8", w % 4)))
                fr["qa", w % 2] = [ev]

                def send(e):
                    r = base_reg(e, ba2i[0:1, w:w + 1], 8 * (N - 16))
                    return e.dma_start(Adw[bass.ds(r, 128), :], Aw8[:, w % 4, :])
                wrote["aw"] = dma("sp", send, "aw", ev, wrote["aw"], part_done)
                fr["aw8", w % 4] = [wrote["aw"]]

        def spread(y, rows, s, ready):
            ev = op("dve", lambda e: e.bn_stats(st[0:rows, s, :], y), ready)
            ev = op("dve", lambda e: e.bn_aggr(sm[0:rows, s, 0:2], st[0:rows, s, :]), ev)
            return op("act", lambda e: e.activation(sm[0:rows, s, 2:3], sm[0:rows, s, 1:2], ACT.Sqrt, bias=eps[0:rows, 0:1]), ev)

        def scale(y, o, rows, s, ready, *before):
            ev = op("dve", lambda e: e.reciprocal(sm[0:rows, s, 3:4], sm[0:rows, s, 2:3]), ready)
            return op("dve", lambda e: e.tensor_scalar(o, y, sm[0:rows, s, 0:1], sm[0:rows, s, 3:4], ALU.subtract, ALU.mult),
                      ev, *before)

        def send_rows(dst, sem, g, src_, ready):
            def send(e):
                r = base_reg(e, bai[0:1, g:g + 1], N - 128)
                return e.dma_start(dst[bass.ds(r, 128), :], src_)
            wrote[sem] = dma("sp", send, sem, ready, wrote[sem], base_done)
            return wrote[sem]

        xw_in = {}

        def load_xw(g):
            def send(e):
                r = base_reg(e, bai[0:1, g:g + 1], N - 128)
                return e.dma_start(xw[:, g % 2, :], x[bass.ds(r, 128), :])
            xw_in[g] = dma("sp", send, f"xw{g % 2}", base_done, *free(("xw", g % 2)))

        def first_post(g):
            s = g % 2

            def f():
                ev = op("dve", lambda e: e.tensor_tensor(hw[:, s, :], Pg[:, s, :], b1[:, :], ALU.add), pg_at[g], ldw, *free(("hw", s)))
                fr.setdefault(("pg", s), []).append(ev)
                ev = op("act", lambda e: e.activation(h1w[:, s, :], hw[:, s, :], ACT.Relu), ev, *free(("h1w", s)))
                fr["hw", s] = [ev]
                fr["h1w", s] = [send_rows(H1, "h1", g, h1w[:, s, :], ev)]
            return [f]

        def second_post(g):
            s = g % 2
            box = {}

            def a():
                ev = op("dve", lambda e: e.tensor_tensor(hw[:, s, :], Pg[:, s, :], b2[:, :], ALU.add), pg_at[g], *free(("hw", s)))
                fr.setdefault(("pg", s), []).append(ev)
                ev = op("dve", lambda e: e.tensor_tensor(hw[:, s, :], hw[:, s, :], xw[:, s, :], ALU.add), ev, xw_in[g])
                fr["xw", s] = [ev]
                box["std"] = spread(hw[:, s, :], 128, s, ev)

            def a2():
                ev = scale(hw[:, s, :], h1w[:, s, :], 128, s, box["std"], *free(("h1w", s)))
                fr["hw", s] = [ev]
                box["x1"] = ev
                fr["h1w", s] = [send_rows(X1, "x1", g, h1w[:, s, :], ev)]
                if g + 2 < NW:
                    load_xw(g + 2)

            def b():
                Q.wait("pe", box["x1"], *free("tr"))
                for k in range(2):
                    ev = op("pe", lambda e, k=k: e.transpose(bank[1][:, k * 128:(k + 1) * 128], h1w[:, s, k * 128:(k + 1) * 128],
                                                             idn[:, :]), sig=(k == 1))
                fr["h1w", s].append(ev)
                ev = op("act", lambda e: e.copy(xT[:, s, :], bank[1][:, 0:256]), ev, *free(("xT", s)))
                fr["tr"] = [ev]

            def c():
                Q.wait("pe", fr["tr"][0])
                for mo in range(2):
                    for k in range(2):
                        ev = op("pe", lambda e, k=k, mo=mo: e.matmul(bank[1][:, 256 + 128 * mo:384 + 128 * mo],
                                                                     wts[:, 0, k, mo * 128:(mo + 1) * 128],
                                                                     xT[:, s, k * 128:(k + 1) * 128], start=(k == 0), stop=(k == 1)),
                                sig=(k == 1))
                fr["xT", s] = [ev]
                for mo in range(2):
                    def put(e, mo=mo):
                        r = base_reg(e, bai[0:1, g:g + 1], N - 128)
                        return e.activation(hT[:, mo, bass.ds(r, 128)], bank[1][:, 256 + 128 * mo:384 + 128 * mo], ACT.Identity,
                                            bias=bT[:, mo:mo + 1])
                    ev = op("act", put, ev, marks["codes"])
                fr["tr"] = [ev]
                marks["h0"] = ev
            return [a, a2, b, c]

        def apply(layer, g):
            W = (W1, W2)[layer]
            s = g % 2

            def part(n):
                def f():
                    if n == 0:
                        Q.wait("pe", z_at[layer, g], marks["W", layer], *free("p"))
                    for q in range(2 * n, 2 * n + 2):
                        k, r = divmod(q, 8)
                        ev = op("pe", lambda e, q=q, k=k, r=r: e.matmul(bank[0][:, 0:256], ZA[:, s, q, 0:128],
                                                                        W[:, k, r * 256:(r + 1) * 256], start=(q == 0),
                                                                        stop=(g == 0 and q == 15)), sig=(q == 15))
                    if n == 7:
                        fr["za", s] = [ev]
                        fr["W1"] = [ev]
                        if g > 0:
                            ev = op("pe", lambda e: e.matmul(bank[0][:, 0:256], Ew[:, s, :], Pg[:, 1 - s, :], start=False, stop=True),
                                    marks["e1"], pg_at[g - 1])
                            fr["e1", s] = [ev]
                            fr.setdefault(("pg", 1 - s), []).append(ev)
                        ev = op("act", lambda e: e.copy(Pg[:, s, :], bank[0][:, 0:256]), ev, *free(("pg", s)))
                        fr["pg", s] = []
                        fr["p"] = [ev]
                        pg_at[g] = ev
                return f

            def sel():
                if g > 0:
                    marks["e1"] = op("dve", lambda e: e.tensor_scalar(Ew[:, s, :], iot[:, :], pd1[:, g:g + 1], None, ALU.is_equal),
                                     pd_done, *free(("e1", s)))
                part(0)()
            return [sel] + [part(n) for n in range(1, 8)]

        g_sl = [0]

        def clear(g, k):
            o = ZA[:, g % 2, 4 * k:4 * k + 4, :].rearrange("p q c -> p (q c)")
            marks["za", g] = op("act", lambda e: e.copy(o, zero[:, 0:1].to_broadcast([128, 4 * ZC])), zero_done,
                                *free(("za", g % 2)))

        def relational(layer, table, ready, extra):
            todo, sel_at, sel_n = {}, {}, [0]
            Q.wait("pool", ready)
            for t in range(T):
                w, i = divmod(t, TA)
                g, wi = divmod(w, SW)
                n = g_sl[0]
                g_sl[0] += 1
                sl, ss, zb = n % NG, n % NSL, w % 2
                K = edge_rows(t)
                if t == 0:
                    for k in range(4):
                        clear(0, k)
                if t % TW in (24, 25, 26, 27) and g + 1 < NW:
                    clear(g + 1, t % TW - 24)
                ge = dma("pool", lambda e, sl=sl, t=t, K=K: e.indirect_dma_start(
                    G[0:K, sl, :], None, table, bass.IndirectOffsetOnAxis(ap=si[0:K, t:t + 1], axis=0)),
                    f"g{sl}", *free(("g", sl)))
                while sel_n[0] < min(T, t + AHEAD):
                    u = sel_n[0]
                    sel_n[0] += 1
                    us = (n - t + u) % NSL
                    sel_at[u] = op("dve", lambda e, us=us, u=u: e.tensor_scalar(S[:, us, :], iot[:, :], c2[:, u:u + 1], wgt[:, u:u + 1],
                                                                                ALU.is_equal, ALU.mult), c2_done, *free(("s", us)))
                se = sel_at[t]
                ev = op("pe", lambda e, sl=sl, ss=ss, i=i, K=K, zb=zb: e.matmul(
                    bank[2 + zb][:, 0:256], S[0:K, ss, :], G[0:K, sl, :], start=(i == 0), stop=(i == TA - 1)),
                    ge, se, *(free(("z", zb)) if i == 0 else []))
                fr["g", sl] = fr["s", ss] = [ev]
                if i == TA - 1:
                    ev = op("act", lambda e, zb=zb: e.copy(Zs[:, zb, :], bank[2 + zb][:, 0:256]), ev, *free(("zs", zb)))
                    fr["z", zb] = [ev]

                    def turn(w=w, g=g, zb=zb, ev=ev, wi=wi):
                        Q.wait("pe", ev, idn_done, *free(("zt", zb)))
                        for k in range(2):
                            e2 = op("pe", lambda e, k=k: e.transpose(bank[4 + zb][:, k * 128:(k + 1) * 128],
                                                                     Zs[:, zb, k * 128:(k + 1) * 128], idn[:, :]), sig=(k == 1))
                        fr["zs", zb] = [e2]

                        def add(e):
                            r = base_reg(e, off[0:1, w:w + 1], 127)
                            o = ZA[:, g % 2, :, bass.ds(r, 16)]
                            return e.tensor_tensor(o, o, bank[4 + zb][:, 0:256].rearrange("p (q c) -> p q c", c=16), ALU.add)
                        z_at[layer, g] = op("dve", add, e2, marks["za", g] if wi == 0 else z_at[layer, g], off_done)
                        fr["zt", zb] = [z_at[layer, g]]
                    todo.setdefault(t + 2, []).append(turn)
                    if wi == SW - 1 or t == T - 1:
                        start, by = (41, 1) if layer == 0 and g == 0 else (t + 4, 2 if g < NW - 2 else 1)
                        post = first_post(g) if layer == 0 else second_post(g)
                        for k, f in enumerate(apply(layer, g) + [lambda: None] + post):
                            todo.setdefault(start + by * k, []).append(f)
                for f in todo.pop(t, []):
                    f()
                extra(layer, t)
            for t in sorted(todo):
                for f in todo[t]:
                    f()

        state = {"a": 0, "load": 0, "deg": 0}
        dsum = {}

        def degree_sum():
            c = state["deg"]
            if c < N // DG:
                state["deg"] += 1
                a = A_sb[0:PB, :, c * DG:(c + 1) * DG].rearrange("p j n -> p n j")
                dsum[c * DG // CH] = op("dve", lambda e: e.tensor_reduce(rdeg[0:PB, c * DG:(c + 1) * DG], a, AX, ALU.add), marks["A"])

        def extra(layer, t):
            n = layer * T + t
            if layer == 0:
                for _ in range(min(len(chores), 1 + (t % 3 != 0) if t < 40 else 1 - t % 2)):
                    chores.pop(0)()
            while state["a"] < T and n >= 90 + state["a"] * 1.65:
                adjacency_tile(state["a"])
                state["a"] += 1
            if n > 1158 and n % 3 == 0 and state["load"] < JB:
                j = state["load"]
                state["load"] += 1
                marks["A"] = dma("act", lambda e: e.dma_start(A_sb[0:PB, j, :], Ad[j * PB:(j + 1) * PB, 0:N]), "ar",
                                 wrote["aw"], marks["W", 1], *free("W1"))

            if n > 1230 and n % 4 == 0:
                degree_sum()

        relational(0, x, ldb, extra)
        assert not chores
        w1_read = fr["W1"]
        load_xw(0)
        load_xw(1)
        relational(1, H1, wrote["h1"], extra)
        assert state["a"] == T and state["load"] == JB

        over = [(k, Q.n[k]) for k in ("pe", "act", "dve")] + [wrote["x1"], wrote["aw"]]
        over_pool = list(over)
        bf = {}

        def bfree(b):
            return [bf[b]] if b in bf else []

        hs_read = [None]
        hs_at = [None] * JB
        h_at = [marks["h0"]] * NC
        rd = [None] * NC
        ar_read = [None] * NR
        cnt = {"nm": 0, "ar": 0}

        def node_major(j):
            b = (6, 7, 2, 3)[cnt["nm"] % 4]
            cnt["nm"] += 1
            Q.wait("pe", h_at[j // 4], *bfree(b))
            for k in range(2):
                ev = op("pe", lambda e, k=k: e.transpose(bank[b][0:PB, k * 128:(k + 1) * 128], hT[:, k, j * PB:(j + 1) * PB],
                                                         idn[:, :]), sig=(k == 1))
            ev = op("act", lambda e: e.copy(hs[0:PB, j, 0, :], bank[b][0:PB, 0:256]), ev, hs_read[0], *over)
            ev = op("dve", lambda e: e.tensor_tensor(hs[0:PB, j, 1, :], bank[b][0:PB, 0:256], hs[0:PB, j, 0, :].bitcast(F32),
                                                     ALU.subtract), ev, hs_read[0], *over)
            bf[b] = ev
            hs_at[j] = ev

        ar_at = {}

        def convert(n):
            l, q = divmod(n, NC * JB)
            c, j = divmod(q, JB)
            sl = n % NR
            i_ = A_sb[0:PB, j, c * CH:(c + 1) * CH]
            o = Ar[0:PB, sl, :]
            if l == 0 or n % 2:
                ar_at[n] = op("act", lambda e: e.copy(o, i_), ar_read[sl], marks["A"], *over)
            else:
                ar_at[n] = op("dve", lambda e: e.tensor_copy(o, i_), ar_read[sl], marks["A"], *over)

        def degree(c):
            rc = rdeg[:, c * CH:(c + 1) * CH]
            ev = op("pe", lambda e: e.matmul(bank[5][:, 0:CH], onef[0:PB, :], rc[0:PB, :], start=True, stop=True), dsum[c], *bfree(5))
            ev = op("dve", lambda e: e.tensor_scalar(rc, bank[5][:, 0:CH], 1.0, None, ALU.max), ev)
            bf[5] = ev
            rd[c] = op("dve", lambda e: e.reciprocal(rc, rc), ev)

        def aggregate(l, c, beside):
            s = c % 2
            bs = [2 * s, 2 * s + 1]
            for b in bs:
                Q.wait("pe", *bfree(b))
            for j in range(JB):
                n = (l * NC + c) * JB + j
                while cnt["ar"] < min(3 * NC * JB, n + 7):
                    convert(cnt["ar"])
                    cnt["ar"] += 1
                beside(j)
                Q.wait("pe", ar_at[n], hs_at[j])
                o = Ar[0:PB, n % NR, :]
                for mo in range(2):
                    for q in range(2):
                        ev = op("pe", lambda e, mo=mo, q=q, j=j, o=o: e.matmul(
                            bank[bs[mo]][:, 0:CH], hs[0:PB, j, q, mo * 128:(mo + 1) * 128], o,
                            start=(j == 0 and q == 0), stop=(j == JB - 1 and q == 1)), sig=(mo == 1 and q == 1))
                ar_read[n % NR] = ev
            while cnt["ar"] < min(3 * NC * JB, n + 8):
                convert(cnt["ar"])
                cnt["ar"] += 1
            hs_read[0] = ev
            rc = rdeg[:, c * CH:(c + 1) * CH]
            for mo in range(2):
                ev = op("dve", lambda e, mo=mo: e.tensor_tensor(agT[:, s, mo, :], bank[bs[mo]][:, 0:CH], rc, ALU.mult),
                        ev if mo == 0 else None, rd[c], fr.get(("ag", s)), *over)
                bf[bs[mo]] = ev
            return ev

        def combine(l, c, ready):
            s = c % 2
            for mo in range(2):
                b = 4 + mo
                Q.wait("pe", *bfree(b), ready, h_at[c])
                for k in range(4):
                    w_ = wts[:, 2 + 2 * l - k // 2, k % 2, mo * 128:(mo + 1) * 128]
                    r_ = hT[:, k % 2, c * CH:(c + 1) * CH] if k < 2 else agT[:, s, k % 2, :]
                    ev = op("pe", lambda e, b=b, w_=w_, r_=r_, k=k: e.matmul(bank[b][:, 0:CH], w_, r_, start=(k == 0), stop=(k == 3)),
                            sig=(k == 3))
            fr["ag", s] = ev
            for mo in range(2):
                b = 4 + mo
                ev2 = op("act", lambda e, b=b, mo=mo: e.activation(hT[:, mo, c * CH:(c + 1) * CH], bank[b][:, 0:CH], ACT.Relu,
                                                                   bias=bT[:, 2 + 2 * l + mo:3 + 2 * l + mo]), ev)
                bf[b] = ev2
            h_at[c] = ev2

        lx = {}
        xr = [None] * 4
        o_free = [None] * 4

        def load_x1(j):
            lx[j] = dma("sp", lambda e: e.dma_start(x1b[0:PB, j % 4, :], X1[j * PB:(j + 1) * PB, :]), f"xs{j % 4}", xr[j % 4], *over)

        def output(j):
            s = j % 4
            b = 6 + j % 2
            Q.wait("pe", h_at[j // 4], *bfree(b))
            for k in range(2):
                ev = op("pe", lambda e, k=k: e.matmul(bank[b][0:PB, 0:256], hT[:, k, j * PB:(j + 1) * PB], wts[:, 7, k, :],
                                                      start=(k == 0), stop=(k == 1)), sig=(k == 1))
            y, o = yb[0:PB, s, :], ob[0:PB, s, :]
            ev = op("dve", lambda e: e.tensor_tensor(y, bank[b][0:PB, 0:256], bo[0:PB, :], ALU.add), ev)
            bf[b] = ev
            ev = op("dve", lambda e: e.tensor_tensor(y, y, x1b[0:PB, s, :], ALU.add), ev, lx[j])
            xr[s] = ev
            if j + 4 < JB:
                load_x1(j + 4)
            std[j] = spread(y, PB, s, ev)

        std = {}

        def output_end(j):
            s = j % 4
            y, o = yb[0:PB, s, :], ob[0:PB, s, :]
            ev = scale(y, o, PB, s, std[j], o_free[s])
            o_free[s] = dma("sp", lambda e: e.dma_start(out[j * PB:(j + 1) * PB, :], o), f"o{s}", ev)

        for j in range(4):
            load_x1(j)
        early = 0
        for l in range(3):
            made = [early]
            ag = {}
            for c in range(NC):
                def beside(j, l=l, c=c):
                    if c == 0:
                        while made[0] < min(JB, j + 4):
                            node_major(made[0])
                            made[0] += 1
                    if l == 0 and j % 3 == 1:
                        degree_sum()
                    if l == 0 and j == 17:
                        degree(c)
                    if l == 2 and c > 1:
                        if j % 5 == 1:
                            output(4 * (c - 2) + j // 5)
                        if j % 5 == 4:
                            output_end(4 * (c - 2) + j // 5)
                ag[c] = aggregate(l, c, beside)
                if c > 0:
                    combine(l, c - 1, ag[c - 1])
            early = 0
            if l < 2:
                while early < 8:
                    node_major(early)
                    early += 1
            combine(l, NC - 1, ag[NC - 1])
            if l < 2:
                while early < 14:
                    node_major(early)
                    early += 1
        for j in range(12, JB):
            output(j)
            if j > 12:
                output_end(j - 1)
        output_end(JB - 1)
        Q.wait("sp", *o_free)

        block = ctx.enter_context(nc.Block())

        def run(eng, e):
            for f in Q.ops[eng][:head[eng]]:
                f(e)
            e.wait_ge(sems["dve"], flag_done[1])
            fast = e.value_load(flag[0:1, 0:1], min_val=0, max_val=1)
            with e.If(fast):
                for f in Q.ops[eng][head[eng]:]:
                    f(e)
            with e.Else():
                if eng == "dve":
                    for name, n in all_done:
                        if n:
                            e.wait_ge(sems[name], n)
                    e.sem_inc(sems["k_" + relay.first(relay.top[0])], 1)
                relay.emit(eng, e, relay.top, None, {})

        @block.tensor
        def _(e):
            run("pe", e)

        @block.scalar
        def _(e):
            run("act", e)

        @block.vector
        def _(e):
            run("dve", e)

        @block.gpsimd
        def _(e):
            run("pool", e)

        @block.sync
        def _(e):
            run("sp", e)


def kernel(x, src, dst, edge_type_8, edge_weight1, L0_gnn_basis, L0_gnn_coeff, L0_gnn_bias, L1_gnn_W_in, L1_gnn_b_in,
           L1_gnn_W_agg, L1_gnn_W_self, L1_gnn_b_hid, L1_gnn_W_out, L1_gnn_b_out):
    import numpy as np
    import concourse.bacc as bacc
    from concourse import mybir as mb
    from concourse.bass_utils import run_bass_kernel_spmd as run

    def tiles(a, pad):
        a = np.asarray(a).reshape(-1)
        a = np.concatenate([a, np.full(T * 128 - E, pad, a.dtype)])
        return np.ascontiguousarray(a.reshape(T, 128).T)

    dst = np.asarray(dst)
    arrays = {
        "x": np.asarray(x),
        "srcT": tiles(src, 0),
        "dstT": tiles(dst, N - 1),
        "etT": tiles(edge_type_8, 0),
        "wT": tiles(edge_weight1, 0.0),
        "large": np.ascontiguousarray(dst[::TW * 128].reshape(1, NW)),
        "small": np.ascontiguousarray(dst[::TA * 128].reshape(1, NA)),
        "basis": np.asarray(L0_gnn_basis),
        "coeff": np.asarray(L0_gnn_coeff).reshape(1, 128),
        "bias": np.asarray(L0_gnn_bias),
        "W_in": np.asarray(L1_gnn_W_in),
        "b_cols": np.ascontiguousarray(np.concatenate([np.asarray(L1_gnn_b_in).reshape(2, 128),
                                                       np.asarray(L1_gnn_b_hid).reshape(6, 128)]).T),
        "b_rows": np.concatenate([np.asarray(L1_gnn_b_in).reshape(1, D), np.asarray(L1_gnn_b_hid)]).reshape(1, 4 * D),
        "W_agg": np.asarray(L1_gnn_W_agg),
        "W_self": np.asarray(L1_gnn_W_self),
        "W_out": np.asarray(L1_gnn_W_out),
        "b_out": np.asarray(L1_gnn_b_out).reshape(1, D),
    }
    arrays = {k: np.ascontiguousarray(v) for k, v in arrays.items()}
    nc = bacc.Bacc("TRN2", target_bir_lowering=False, num_devices=1)
    h = {k: nc.dram_tensor("in_" + k, v.shape, mb.dt.from_np(v.dtype), kind="ExternalInput").ap() for k, v in arrays.items()}
    o = nc.dram_tensor("out", (N, D), mb.dt.float32, kind="ExternalOutput").ap()
    program(nc, h["x"], h["srcT"], h["dstT"], h["etT"], h["wT"], h["large"], h["small"], h["basis"], h["coeff"], h["bias"],
            h["W_in"], h["b_cols"], h["W_agg"], h["W_self"], h["b_rows"], h["W_out"], h["b_out"], o)
    r = run(nc, [{"in_" + k: v for k, v in arrays.items()}], core_ids=[0])
    return r.results[0]["out"]
```

```python
from contextlib import ExitStack

import concourse.bass as bass
from concourse import mybir

F32 = mybir.dt.float32
BF16 = mybir.dt.bfloat16
F32R = mybir.dt.float32r
U8 = mybir.dt.uint8
F16 = mybir.dt.float16
I32 = mybir.dt.int32
ALU = mybir.AluOpType
ACT = mybir.ActivationFunctionType
AX = mybir.AxisListType.X
RMAX = bass.bass_isa.ReduceOp.max

N = 2500
D = 256
E = 82500
R = 8
T = 645
LASTP = E - (T - 1) * 128
TA = 3
NA = 215
SW = 10
TW = SW * TA
NW = 22
ZC = 144
NB = 320
NS = 8 * NB
JB = 20
PB = 125
CH = 500
NC = 5
NG = 16
NSL = 8
AHEAD = 6
NR = 8
AHEAD_HS = 8
FIRST = 12
WPE = 2
DG = 100
EPS = 1e-5


class Queues:

    def __init__(self, sems):
        self.ops = {e: [] for e in ("pe", "act", "dve", "pool", "sp")}
        self.sems = sems
        self.n = {}
        self.seen = {}

    def wait(self, eng, *events):
        for ev in events:
            if ev is None:
                continue
            sem, v = ev
            if self.seen.get((eng, sem), 0) < v:
                self.seen[(eng, sem)] = v
                self.ops[eng].append(lambda e, s=self.sems[sem], v=v: e.wait_ge(s, v))

    def op(self, eng, fn, *events, sig=True):
        self.wait(eng, *events)
        if not sig:
            self.ops[eng].append(fn)
            return None
        s = self.sems[eng]
        self.ops[eng].append(lambda e: fn(e).then_inc(s, 1))
        self.n[eng] = self.n.get(eng, 0) + 1
        return eng, self.n[eng]

    def dma(self, eng, fn, sem, *events):
        self.wait(eng, *events)
        s = self.sems[sem]
        self.ops[eng].append(lambda e: fn(e).then_inc(s, 16))
        self.n[sem] = self.n.get(sem, 0) + 16
        return sem, self.n[sem]


class Names:
    pass


class Relay:

    def __init__(self, sems):
        self.sems = sems
        self.top = []
        self.at = [self.top]

    def step(self, eng, fn):
        self.at[-1].append((eng, fn))

    def loop(self, name, count, fill):
        body = []
        self.at[-1].append((None, name, count, body))
        self.at.append(body)
        fill()
        self.at.pop()

    def first(self, item):
        return item[0] or self.first(item[3][0])

    def engines(self, body):
        got = set()
        for item in body:
            got |= {item[0]} if item[0] else self.engines(item[3])
        return got

    def emit(self, eng, e, body, after, v):
        for n, item in enumerate(body):
            nxt = self.first(body[n + 1]) if n + 1 < len(body) else after
            if item[0] is None:
                _, name, count, inner = item
                assert nxt in (None, self.first(inner[0]))
                if eng in self.engines(inner):
                    with e.Fori(0, count) as i:
                        self.emit(eng, e, inner, self.first(inner[0]), {**v, name: i})
            elif item[0] == eng:
                own = self.sems["k_" + eng]
                e.wait_ge(own, 1)
                e.sem_clear(own)
                give = self.sems["k_" + (nxt or "end")]
                if eng == "sp":
                    item[1](e, v).then_inc(self.sems["k_dma"], 16)
                    e.wait_ge(self.sems["k_dma"], 16)
                    e.sem_clear(self.sems["k_dma"])
                    e.sem_inc(give, 1)
                elif eng == "pool":
                    item[1](e, v).then_inc(self.sems["k_gather"], 16)
                    e.drain().then_inc(give, 1)
                else:
                    item[1](e, v).then_inc(give, 1)


def general(relay, m):
    dve, act, pe, sp, pool = (lambda fn, g=g: relay.step(g, fn) for g in ("dve", "act", "pe", "sp", "pool"))

    def rows(ap, v):
        return ap[bass.ds(v["k"] * PB, PB), :]

    def sums(table, index, key, weight):
        dve(lambda e, v: e.memset(m.acc, 0.0))

        def tile():
            dve(lambda e, v: e.tensor_copy(m.ix, index[:, bass.ds(v["t"], 1)]))
            dve(lambda e, v: e.tensor_copy(m.dw[:, 0:1], key[:, bass.ds(v["t"], 1)]))
            dve(lambda e, v: e.tensor_copy(m.dw[:, 1:2], weight[:, bass.ds(v["t"], 1)]))
            dve(lambda e, v: e.tensor_tensor(m.dw[:, 0:1], m.dw[:, 0:1], m.base, ALU.subtract))
            dve(lambda e, v: e.tensor_scalar(m.S, m.iot, m.dw[:, 0:1], m.dw[:, 1:2], ALU.is_equal, ALU.mult))
            pool(lambda e, v: e.indirect_dma_start(m.G, None, table, bass.IndirectOffsetOnAxis(ap=m.ix, axis=0)))
            pe(lambda e, v: e.matmul(m.bank[0][:, 0:256], m.S, m.G, start=True, stop=True))
            pe(lambda e, v: e.matmul(m.bank[1][:, 0:1], m.S, m.onef, start=True, stop=True))
            dve(lambda e, v: e.tensor_tensor(m.acc[:, 0:256], m.acc[:, 0:256], m.bank[0][:, 0:256], ALU.add))
            dve(lambda e, v: e.tensor_tensor(m.acc[:, 256:257], m.acc[:, 256:257], m.bank[1][:, 0:1], ALU.add))

        relay.loop("t", T, tile)

    def turned(src, dst):
        for k in range(2):
            pe(lambda e, v, k=k: e.transpose(m.bank[2][:, k * 128:k * 128 + PB], src[0:PB, k * 128:(k + 1) * 128], m.idn[0:PB, 0:PB]))
        act(lambda e, v: e.copy(dst[:, :, 0:PB], m.bank[2][:, 0:256].rearrange("p (k n) -> p k n", n=128)[:, :, 0:PB]))

    def product(pairs, cols=256):
        n = 2 * len(pairs)
        for i, (hT_, w_) in enumerate(pairs):
            for k in range(2):
                pe(lambda e, v, hT_=hT_, w_=w_, k=k, i=i: e.matmul(m.bank[3][0:PB, 0:cols], hT_[:, k, 0:PB], w_[:, k, :],
                                                                   start=(i == 0 and k == 0), stop=(2 * i + k == n - 1)))

    def norm(y, o):
        dve(lambda e, v: e.bn_stats(m.st[0:PB, 0, :], y[0:PB, :]))
        dve(lambda e, v: e.bn_aggr(m.sm[0:PB, 0, 0:2], m.st[0:PB, 0, :]))
        act(lambda e, v: e.activation(m.sm[0:PB, 0, 2:3], m.sm[0:PB, 0, 1:2], ACT.Sqrt, bias=m.eps[0:PB, 0:1]))
        dve(lambda e, v: e.reciprocal(m.sm[0:PB, 0, 3:4], m.sm[0:PB, 0, 2:3]))
        dve(lambda e, v: e.tensor_scalar(o[0:PB, :], y[0:PB, :], m.sm[0:PB, 0, 0:1], m.sm[0:PB, 0, 3:4], ALU.subtract, ALU.mult))

    def blocks(fill):
        dve(lambda e, v: e.memset(m.base, 0.0))

        def body():
            fill()
            dve(lambda e, v: e.tensor_scalar(m.base, m.base, float(PB), None, ALU.add))
        relay.loop("k", JB, body)

    def table():
        dve(lambda e, v: e.memset(m.z, 0.0))
        sp(lambda e, v: e.dma_start(m.z[0:PB, :], rows(m.x, v)))
        turned(m.z, m.hT)
        row(m.W1)
        sp(lambda e, v: e.dma_start(rows(m.T1, v), m.row[0:PB, :]))

    def row(W):
        for c in range(4):
            product([(m.hT, W[:, :, c * 512:(c + 1) * 512])], 512)
            act(lambda e, v, c=c: e.copy(m.row[0:PB, c * 512:(c + 1) * 512], m.bank[3][0:PB, :]))

    def first():
        sums(m.T1g, m.idx, m.df, m.wgt)
        dve(lambda e, v: e.tensor_tensor(m.y, m.acc[:, 0:256], m.b1, ALU.add))
        dve(lambda e, v: e.tensor_scalar(m.y, m.y, 0.0, None, ALU.max))
        turned(m.y, m.hT)
        row(m.W2)
        sp(lambda e, v: e.dma_start(rows(m.T2, v), m.row[0:PB, :]))

    def second():
        sums(m.T2g, m.idx, m.df, m.wgt)
        dve(lambda e, v: e.tensor_tensor(m.y, m.acc[:, 0:256], m.b2, ALU.add))
        sp(lambda e, v: e.dma_start(m.z[0:PB, :], rows(m.x, v)))
        dve(lambda e, v: e.tensor_tensor(m.y[0:PB, :], m.y[0:PB, :], m.z[0:PB, :], ALU.add))
        norm(m.y, m.z)
        sp(lambda e, v: e.dma_start(rows(m.X1, v), m.z[0:PB, :]))
        turned(m.z, m.hT)
        product([(m.hT, m.wts[:, 0, :, :])])
        dve(lambda e, v: e.tensor_tensor(m.y[0:PB, :], m.bank[3][0:PB, 0:256], m.brow4[0:PB, 0, :], ALU.add))
        sp(lambda e, v: e.dma_start(rows(m.H[0], v), m.y[0:PB, :]))

    def sage(l):
        def f():
            sums(m.H[l], m.di, m.sf, m.wone)
            dve(lambda e, v: e.tensor_scalar(m.acc[:, 256:257], m.acc[:, 256:257], 1.0, None, ALU.max))
            sp(lambda e, v: e.dma_start(m.z[0:PB, :], rows(m.H[l], v)))
            dve(lambda e, v: e.reciprocal(m.acc[:, 256:257], m.acc[:, 256:257]))
            dve(lambda e, v: e.tensor_scalar(m.y, m.acc[:, 0:256], m.acc[:, 256:257], None, ALU.mult))
            turned(m.y, m.hT)
            turned(m.z, m.hT2)
            product([(m.hT, m.wts[:, 1 + 2 * l, :, :]), (m.hT2, m.wts[:, 2 + 2 * l, :, :])])
            dve(lambda e, v: e.tensor_tensor(m.y[0:PB, :], m.bank[3][0:PB, 0:256], m.brow4[0:PB, 1 + l, :], ALU.add))
            dve(lambda e, v: e.tensor_scalar(m.y, m.y, 0.0, None, ALU.max))
            sp(lambda e, v: e.dma_start(rows(m.H[l + 1], v), m.y[0:PB, :]))
        return f

    def last():
        sp(lambda e, v: e.dma_start(m.z[0:PB, :], rows(m.H[3], v)))
        turned(m.z, m.hT)
        product([(m.hT, m.wts[:, 7, :, :])])
        sp(lambda e, v: e.dma_start(m.z[0:PB, :], rows(m.X1, v)))
        dve(lambda e, v: e.tensor_tensor(m.y[0:PB, :], m.bank[3][0:PB, 0:256], m.bo[0:PB, :], ALU.add))
        dve(lambda e, v: e.tensor_tensor(m.y[0:PB, :], m.y[0:PB, :], m.z[0:PB, :], ALU.add))
        norm(m.y, m.z)
        sp(lambda e, v: e.dma_start(rows(m.out, v), m.z[0:PB, :]))

    dve(lambda e, v: e.memset(m.onef, 1.0))
    dve(lambda e, v: e.tensor_copy(m.df, m.di))
    dve(lambda e, v: e.tensor_copy(m.sf, m.si))
    dve(lambda e, v: e.tensor_scalar(m.t_, m.sf, 8.0, None, ALU.mult))
    dve(lambda e, v: e.tensor_copy(m.wone, m.ei))
    dve(lambda e, v: e.tensor_tensor(m.t_, m.t_, m.wone, ALU.add))
    dve(lambda e, v: e.tensor_copy(m.idx, m.t_))
    for l, W in ((0, m.W1), (1, m.W2)):
        for r in range(R):
            for b in range(R):
                o = W[:, :, r * 256:(r + 1) * 256]
                c = m.cf[:, l * 64 + r * 8 + b:l * 64 + r * 8 + b + 1]
                i_ = m.bas[l][:, b, :, :]
                if b == 0:
                    dve(lambda e, v, o=o, c=c, i_=i_: e.tensor_scalar(o, i_, c, None, ALU.mult))
                else:
                    dve(lambda e, v, o=o, c=c, i_=i_: e.scalar_tensor_tensor(o, i_, c, o, ALU.mult, ALU.add))
    sp(lambda e, v: e.dma_start(m.brow, m.b_rows.to_broadcast([128, 4 * D])))
    dve(lambda e, v: e.memset(m.wone, 1.0))
    dve(lambda e, v: e.tensor_scalar(m.wone[:, T - 1:T], m.ip, float(LASTP), None, ALU.is_lt))
    for f in (table, first, second, sage(0), sage(1), sage(2)):
        blocks(f)
    dve(lambda e, v: e.memset(m.base, 0.0))

    def body():
        dve(lambda e, v: e.memset(m.base, 0.0))
        last()
    relay.loop("k", JB, body)
    dve(lambda e, v: e.memset(m.base, 0.0))


def program(nc, x, srcT, dstT, etT, wT, large, small, basis, coeff, bias, W_in, b_in, W_agg, W_self,
            b_rows, W_out, b_out, out):
    def dram(name, shape, dt=F32):
        return nc.dram_tensor(name, shape, dt, kind="Internal").ap()

    H1 = dram("H1", (N, D))
    X1 = dram("X1", (N, D))
    Ad = dram("Ad", (N, NS), U8)
    T1, T2 = dram("T1", (N, R * D)), dram("T2", (N, R * D))
    H = [dram(f"H{i}_", (N, D)) for i in range(4)]

    with ExitStack() as ctx:
        def sb(n, s, d):
            return ctx.enter_context(nc.sbuf_tensor(n, s, d))

        names = (["pe", "act", "dve", "pool"] + [f"g{i}" for i in range(NG)]
                 + ["src", "edge", "base", "wts", "bas0", "bas1", "aw", "h1", "x1", "xw0", "xw1", "ar", "k_pe", "k_act", "k_dve",
                    "k_pool", "k_sp", "k_end", "k_dma", "k_gather"] + [f"xs{i}" for i in range(4)] + [f"o{i}" for i in range(4)])
        sems = {n: ctx.enter_context(nc.semaphore("s_" + n)) for n in names}
        Q = Queues(sems)
        op, dma = Q.op, Q.dma
        size = {F32: 4, I32: 4, BF16: 2, F16: 2, U8: 1}

        def lay(reg, *items):
            off, got = 0, []
            for shape, dt in items:
                n = 1
                for s in shape:
                    n *= s
                nb = (n * size[dt] + 31) // 32 * 32
                assert off + nb <= reg.shape[1] * 4, (shape, off + nb)
                v = reg[:, off // 4:(off + nb) // 4]
                v = (v if dt == F32 else v.bitcast(dt))[:, 0:n]
                if len(shape) == 2:
                    v = v.rearrange("p (a b) -> p a b", b=shape[1])
                elif len(shape) == 3:
                    v = v.rearrange("p (a b c) -> p a b c", b=shape[1], c=shape[2])
                got.append(v)
                off += nb
            return got

        wts = sb("wts", [128, 8, 2, 256], F32)
        idn = sb("idn", [128, 128], F32)
        onef = sb("onef", [128, 128], F32)
        iot = sb("iot", [128, 128], F32)
        iotN = sb("iotN", [128, NB], F16)
        ip = sb("ip", [128, 1], F32)
        eps = sb("eps", [128, 1], F32)
        zero = sb("zero", [128, 1], F32)
        b1 = sb("b1", [128, 256], F32)
        b2 = sb("b2", [128, 256], F32)
        bo = sb("bo", [128, 256], F32)
        bT = sb("bT", [128, 8], F32)
        cf = sb("cf", [128, 128], F32)
        c1 = sb("c1", [128, T], F32)
        bcol = sb("bcol", [128, T], F32)
        c2 = sb("c2", [128, T], F32)
        wgt = sb("wgt", [128, T], F32)
        di = sb("di", [128, T], I32)
        si = sb("si", [128, T], I32)
        ei = sb("ei", [128, T], I32)
        ba = sb("ba", [128, NW], F32)
        bai = sb("bai", [128, NW], I32)
        pd1 = sb("pd1", [128, NW], F32)
        ba2 = sb("ba2", [128, NA], F32)
        ba2i = sb("ba2i", [128, NA], I32)
        pd2 = sb("pd2", [128, NA], F32)
        off = sb("off", [128, NA], I32)
        chk = sb("chk", [128, 16], F32)
        flag = sb("flag", [128, 1], I32)
        st = sb("st", [128, 4, 6], F32)
        sm = sb("sm", [128, 4, 4], F32)
        rdeg = sb("rdeg", [128, N], F32)
        hT = sb("hT", [128, 2, N], F32)
        RX = sb("RX", [128, 12800], F32)
        bas0, bas1, W1 = lay(RX, ((8, 2, 256), F32), ((8, 2, 256), F32), ((2, 2048), F32))
        bas = [bas0, bas1]
        A_sb = lay(RX, ((JB, N), U8))[0]
        df, sf, dl, aq = lay(hT[:, :, :].rearrange("p k n -> p (k n)"), *[((T,), F32)] * 4)
        with ExitStack() as inner:
            RY = inner.enter_context(nc.sbuf_tensor("RY", [128, 20480], F32))
        (Mr, Nr, Aw, Aw8, E2, G, S, Zs, W2, ZA, Ew, Pg, hw, h1w, xw, xT) = lay(
            RY, ((NSL, 128), BF16), ((NSL, NB), BF16), ((4, NB), BF16), ((4, NB), U8), ((2, 128), BF16), ((NG, 256), F32),
            ((NSL, 128), F32), ((2, 256), F32), ((2, 2048), F32), ((2, 16 * ZC), F32), ((2, 128), F32), ((2, 256), F32),
            ((2, 256), F32), ((2, 256), F32), ((2, 256), F32), ((2, 256), F32))
        ZA = ZA.rearrange("p s (q c) -> p s q c", c=ZC)
        Ar = sb("Ar", [128, NR, CH], F32R)
        hs = sb("hs", [128, JB, 2, 256], F32R)
        agT = sb("agT", [128, 2, 2, CH], F32)
        yb = sb("yb", [128, 4, 256], F32)
        ob = sb("ob", [128, 4, 256], F32)
        x1b = sb("x1b", [128, 4, 256], F32)

        bank = [ctx.enter_context(nc.psum_tensor(f"bank{i}", [128, 512], F32)) for i in range(8)]

        lds = dma("act", lambda e: e.dma_start(si[:, :], srcT), "src")
        for t_, s_ in ((di, dstT), (ei, etT), (wgt, wT)):
            ld = dma("sp", lambda e, t_=t_, s_=s_: e.dma_start(t_[:, :], s_), "edge")
        dma("act", lambda e: e.dma_start(ba2i[:, :], small.to_broadcast([128, NA])), "base")
        ldb = dma("act", lambda e: e.dma_start(bai[:, :], large.to_broadcast([128, NW])), "base")
        dma("act", lambda e: e.dma_start(cf[:, :], coeff.to_broadcast([128, 128])), "bas0")
        ldbas = [dma("act", lambda e, l=l: e.dma_start(bas[l], basis[l].rearrange("b (k p) o -> p b k o", p=128)), f"bas{l}")
                 for l in range(2)]
        for i, w in enumerate([W_in, W_agg[0], W_self[0], W_agg[1], W_self[1], W_agg[2], W_self[2], W_out]):
            dma("sp", lambda e, i=i, w=w: e.dma_start(wts[:, i, :, :], w.rearrange("(k p) o -> p k o", p=128)), "wts")
        for t_, s_ in ((b1, bias[0:1, :]), (b2, bias[1:2, :]), (bo, b_out)):
            dma("sp", lambda e, t_=t_, s_=s_: e.dma_start(t_[:, :], s_.to_broadcast([128, 256])), "wts")
        ldw = dma("sp", lambda e: e.dma_start(bT[:, :], b_in), "wts")

        def iota(t_, n, step, mult):
            return op("pool", lambda e: e.iota(t_, pattern=[[step, n]], base=0, channel_multiplier=mult,
                                               allow_small_or_imprecise_dtypes=True))

        iota(ip[:, :], 1, 1, 1)
        iota(iot[:, :], 128, 1, 0)
        iot_done = iota(iotN[:, :], NB, 1, 0)

        def dve(fn, *ev):
            return op("dve", fn, *ev)

        dve(lambda e: e.memset(eps[:, :], EPS))
        zero_done = dve(lambda e: e.memset(zero[:, :], 0.0))
        idn_done = dve(lambda e: e.tensor_scalar(idn[:, :], iot[:, :], ip[:, 0:1], None, ALU.is_equal), iot_done)

        def edge_rows(t):
            return 128 if t < T - 1 else LASTP

        def gather(n, t, table, *before):
            K = edge_rows(t)
            return dma("pool", lambda e: e.indirect_dma_start(
                G[0:K, n % NG, :], None, table, bass.IndirectOffsetOnAxis(ap=si[0:K, t:t + 1], axis=0)), f"g{n % NG}", *before)

        gathered = [gather(t, t, x, lds) for t in range(FIRST)]

        Q.wait("dve", ldb, ld)
        dve(lambda e: e.tensor_copy(ba[:, :], bai[:, :]))
        e1 = dve(lambda e: e.tensor_copy(ba2[:, :], ba2i[:, :]))
        df_done = dve(lambda e: e.tensor_copy(df, di[:, :]))
        dve(lambda e: e.tensor_scalar(ba[:, :], ba[:, :], float(N - 128), None, ALU.min), e1)
        ev = dve(lambda e: e.tensor_scalar(ba2[:, :], ba2[:, :], float(N - 16), None, ALU.min))
        dve(lambda e: e.memset(ba[:, 0:1], 0.0), ev)
        dve(lambda e: e.memset(ba[:, NW - 1:NW], float(N - 128)))
        dve(lambda e: e.memset(ba2[:, 0:1], 0.0))
        eb = dve(lambda e: e.memset(ba2[:, NA - 1:NA], float(N - 16)))
        nf = (NW - 1) * TW
        e1 = dve(lambda e: e.tensor_tensor(c1[:, :].rearrange("p (w t) -> p w t", t=TA), df.rearrange("p (w t) -> p w t", t=TA),
                                           ba2[:, :].unsqueeze(2).to_broadcast([128, NA, TA]), ALU.subtract), eb, df_done)
        dve(lambda e: e.tensor_tensor(dl[:, 0:nf].rearrange("p (w t) -> p w t", t=TW),
                                      df[:, 0:nf].rearrange("p (w t) -> p w t", t=TW),
                                      ba[:, 0:NW - 1].unsqueeze(2).to_broadcast([128, NW - 1, TW]), ALU.subtract))
        dve(lambda e: e.tensor_scalar(dl[:, nf:T], df[:, nf:T], ba[:, NW - 1:NW], None, ALU.subtract))
        dve(lambda e: e.tensor_tensor(pd1[:, 1:NW], ba[:, 1:NW], ba[:, 0:NW - 1], ALU.subtract))
        dve(lambda e: e.tensor_tensor(pd2[:, 1:NA], ba2[:, 1:NA], ba2[:, 0:NA - 1], ALU.subtract))
        ev = dve(lambda e: e.tensor_tensor(aq[:, 0:T - 2], df[:, 2:T], df[:, 0:T - 2], ALU.subtract))
        c2_done = dve(lambda e: e.scalar_tensor_tensor(c2[:, :], ei[:, :], 16.0, c1[:, :], ALU.mult, ALU.add), e1)
        low = [(dl, 0), (c1[:, :], 0), (pd1[:, 1:NW], 0), (pd2[:, 1:NA], 0), (aq[:, 0:T - 2], 1)]
        high = [(dl, 127), (c1[:, :], 15), (pd1[:, 1:NW], 128), (pd2[:, 1:NA], 16)]
        for n, (s_, _) in enumerate(low):
            ev = dve(lambda e, n=n, s_=s_: e.tensor_reduce(chk[:, n:n + 1], s_, AX, ALU.min), ev)
        for n, (s_, _) in enumerate(high):
            ev = dve(lambda e, n=n, s_=s_: e.tensor_reduce(chk[:, 5 + n:6 + n], s_, AX, ALU.max))
        for n, (_, v) in enumerate(low):
            ev = dve(lambda e, n=n, v=v: e.tensor_scalar(chk[:, n:n + 1], chk[:, n:n + 1], -1.0, float(v), ALU.mult, ALU.add), ev)
        for n, (_, v) in enumerate(high):
            ev = dve(lambda e, n=n, v=v: e.tensor_scalar(chk[:, 5 + n:6 + n], chk[:, 5 + n:6 + n], float(-v), None, ALU.add))
        ev = dve(lambda e: e.tensor_reduce(chk[:, 9:10], chk[:, 0:9], AX, ALU.max), ev)
        ev = op("pool", lambda e: e.partition_all_reduce(chk[:, 10:11], chk[:, 9:10], 128, RMAX), ev)
        flag_done = dve(lambda e: e.tensor_scalar(flag[:, :], chk[:, 10:11], 0.0, None, ALU.is_le), ev)

        all_done = [("pe", 0), ("act", 0), ("pool", Q.n["pool"]), ("dve", Q.n["dve"]), ldw, ld, lds, ldb, *ldbas, *gathered]
        head = {k: len(v) for k, v in Q.ops.items()}
        m = Names()
        m.T1g = T1.rearrange("n (r o) -> (n r) o", o=D)
        m.T2g = T2.rearrange("n (r o) -> (n r) o", o=D)
        m.T1, m.T2, m.X1, m.H, m.x, m.out, m.b_rows = T1, T2, X1, H, x, out, b_rows
        m.wgt, m.di, m.si, m.ei = wgt[:, :], di[:, :], si[:, :], ei[:, :]
        m.ip, m.iot, m.idn, m.b1, m.b2, m.bo, m.W1, m.wts = ip[:, :], iot[:, :], idn, b1[:, :], b2[:, :], bo, W1, wts
        m.st, m.sm, m.eps, m.bank, m.cf, m.bas = st, sm, eps, bank, cf, bas
        (m.W2, m.G, m.S, m.acc, m.y, m.z, m.hT, m.hT2, m.wone, m.brow, m.dw, m.onef, m.ix, m.base, m.row, m.df, m.sf, m.t_,
         m.idx) = lay(RY, ((2, 2048), F32), ((256,), F32), ((128,), F32), ((257,), F32), ((256,), F32), ((256,), F32),
                      ((2, 128), F32), ((2, 128), F32), ((T,), F32), ((4 * D,), F32), ((2,), F32), ((1,), F32), ((1,), I32),
                      ((1,), F32), ((2048,), F32), ((T,), F32), ((T,), F32), ((T,), F32), ((T,), I32))
        m.brow4 = m.brow.rearrange("p (l c) -> p l c", c=D)
        relay = Relay(sems)
        general(relay, m)

        e1 = dve(lambda e: e.tensor_copy(ba2i[:, :], ba2[:, :]))
        ev = dve(lambda e: e.tensor_copy(bai[:, :], ba[:, :]))
        base_done = ev
        ns = (NW - 1) * SW
        dve(lambda e: e.tensor_tensor(off[:, 0:ns].rearrange("p (w t) -> p w t", t=SW),
                                      ba2i[:, 0:ns].rearrange("p (w t) -> p w t", t=SW),
                                      bai[:, 0:NW - 1].unsqueeze(2).to_broadcast([128, NW - 1, SW]), ALU.subtract), ev)
        off_done = dve(lambda e: e.tensor_tensor(off[:, ns:NA], ba2i[:, ns:NA], bai[:, NW - 1:NW].to_broadcast([128, NA - ns]),
                                                 ALU.subtract))
        part_done = dve(lambda e: e.tensor_scalar(ba2i[:, :], ba2[:, :], 8.0, None, ALU.mult), off_done)
        dve(lambda e: e.tensor_scalar(pd1[:, 1:NW], pd1[:, 1:NW], -1.0, ip[:, 0:1], ALU.mult, ALU.add))
        pd_done = dve(lambda e: e.tensor_scalar(pd2[:, 1:NA], pd2[:, 1:NA], -8.0, ip[:, 0:1], ALU.mult, ALU.add))
        dve(lambda e: e.memset(onef[:, :], 1.0))

        chores = []
        marks = {}

        def relation_weights(l, W, relations):
            for first in range(0, len(relations), 2):
                last = [None, None]
                for b in range(8):
                    for q, r in enumerate(relations[first:first + 2]):

                        def f(b=b, q=q, r=r, last=last):
                            o = W[:, :, r * 256:(r + 1) * 256]
                            c = cf[:, l * 64 + r * 8 + b:l * 64 + r * 8 + b + 1]
                            i_ = bas[l][:, b, :, :]
                            if b == 0:
                                last[q] = dve(lambda e: e.tensor_scalar(o, i_, c, None, ALU.mult), ldbas[l])
                            else:
                                last[q] = dve(lambda e: e.scalar_tensor_tensor(o, i_, c, o, ALU.mult, ALU.add), last[q])
                            marks["W", l] = last[q]
                        chores.append(f)

        def adjacency_codes():
            box = [None]

            def add(fn):
                def f():
                    box[0] = dve(fn, box[0])
                    marks["codes"] = box[0]
                chores.append(f)
            box[0] = lds
            add(lambda e: e.tensor_copy(sf, si[:, :]))
            add(lambda e: e.tensor_scalar(aq, sf, float(NB), None, ALU.is_ge))
            for q in range(2, 8):
                add(lambda e, q=q: e.scalar_tensor_tensor(aq, sf, float(NB * q), aq, ALU.is_ge, ALU.add))
            add(lambda e: e.scalar_tensor_tensor(c1[:, :], c1[:, :], 8.0, aq, ALU.mult, ALU.add))
            add(lambda e: e.scalar_tensor_tensor(bcol[:, :], aq, float(-NB), sf, ALU.mult, ALU.add))

        relation_weights(0, W1, list(range(WPE, 8)))
        adjacency_codes()
        relation_weights(1, W2, list(range(8)))
        products = []
        diag = [v[:, k, h * 128:(h + 1) * 128] for v in (xw, xT) for k in range(2) for h in range(2)]
        diag_free = [None] * 8
        diag_at = []

        def product(r, b):
            def f():
                n = r * 8 + b
                k = bank[6 + r % 2]
                while len(diag_at) < min(8 * WPE, n + 7):
                    m_ = len(diag_at)
                    diag_at.append(op("act", lambda e, m_=m_: e.activation(diag[m_ % 8], idn[:, :], ACT.Copy, scale=cf[:, m_:m_ + 1]),
                                      diag_free[m_ % 8], idn_done, ldbas[0]))
                ev = diag_at[n]
                if b == 0:
                    Q.wait("pe", marks.get(("wb", r % 2)))
                ev = op("pe", lambda e: e.matmul(k[:, :], diag[n % 8], bas0[:, b, :, :].rearrange("p k o -> p (k o)"), start=(b == 0),
                                                 stop=(b == 7)), ev)
                diag_free[n % 8] = ev
                if b == 7:
                    marks["wb", r % 2] = marks["W1pe"] = op("act", lambda e: e.copy(
                        W1[:, :, r * 256:(r + 1) * 256], k[:, :].rearrange("p (k o) -> p k o", o=256)), ev)
            return f

        for r in range(WPE):
            for b in range(8):
                products.append(product(r, b))

        Adw = Ad.rearrange("d (a b) -> (d a) b", b=NB)
        fr = {}
        z_at = {}
        pg_at, z_ready, aw_at = {}, {}, {}
        wrote = {"h1": None, "x1": None, "aw": None}

        def free(key):
            return fr.get(key, [])

        def base_reg(e, ap, top):
            return e.value_load(ap, min_val=0, max_val=top)

        hot_at, hot_n = {}, [0]

        def adjacency_tile(t):
            w, i = divmod(t, TA)
            sl = t % NSL
            b = bank[6 + w % 2]
            K = edge_rows(t)
            while hot_n[0] < min(T, t + 3):
                u = hot_n[0]
                hot_n[0] += 1
                us = u % NSL
                op("dve", lambda e, u=u, us=us: e.tensor_scalar(Mr[:, us, :], iotN[:, 0:128], c1[:, u:u + 1], None, ALU.is_equal),
                   marks["codes"], *free(("m", us)))
                hot_at[u] = op("dve", lambda e, u=u, us=us: e.tensor_scalar(Nr[:, us, :], iotN[:, :], bcol[:, u:u + 1], None,
                                                                            ALU.is_equal))
            ev = hot_at[t]
            ev = op("pe", lambda e: e.matmul(b[:, 0:NB], Mr[0:K, sl, :], Nr[0:K, sl, :], start=(i == 0),
                                             stop=(w == 0 and i == TA - 1)),
                    ev, *(free(("qa", w % 2)) if i == 0 else []))
            fr["m", sl] = [ev]
            if i == 0 and w > 0:
                marks["e2"] = op("dve", lambda e: e.tensor_scalar(E2[:, w % 2, :], iot[:, :], pd2[:, w:w + 1], None, ALU.is_equal),
                                 pd_done, *free(("e2", w % 2)))
            if i == TA - 1:
                if w > 0:
                    ev = op("pe", lambda e: e.matmul(b[:, 0:NB], E2[:, w % 2, :], Aw[:, (w - 1) % 4, :], start=False, stop=True),
                            marks["e2"], aw_at[w - 1])
                    fr["e2", w % 2] = [ev]
                    fr["aw", (w - 1) % 4] = [ev]
                op("act", lambda e: e.copy(Aw[:, w % 4, :], b[:, 0:NB]), ev, *free(("aw", w % 4)))
                aw_at[w] = ("act", Q.n["act"])
                ev = op("act", lambda e: e.copy(Aw8[:, w % 4, :], b[:, 0:NB]), *free(("aw8", w % 4)))
                fr["qa", w % 2] = [ev]

                def send(e):
                    r = base_reg(e, ba2i[0:1, w:w + 1], 8 * (N - 16))
                    return e.dma_start(Adw[bass.ds(r, 128), :], Aw8[:, w % 4, :])
                wrote["aw"] = dma("sp", send, "aw", ev, wrote["aw"], part_done)
                fr["aw8", w % 4] = [wrote["aw"]]

        def spread(y, rows, s, ready):
            ev = op("dve", lambda e: e.bn_stats(st[0:rows, s, :], y), ready)
            ev = op("dve", lambda e: e.bn_aggr(sm[0:rows, s, 0:2], st[0:rows, s, :]), ev)
            return op("act", lambda e: e.activation(sm[0:rows, s, 2:3], sm[0:rows, s, 1:2], ACT.Sqrt, bias=eps[0:rows, 0:1]), ev)

        def scale(y, o, rows, s, ready, *before):
            ev = op("dve", lambda e: e.reciprocal(sm[0:rows, s, 3:4], sm[0:rows, s, 2:3]), ready)
            return op("dve", lambda e: e.tensor_scalar(o, y, sm[0:rows, s, 0:1], sm[0:rows, s, 3:4], ALU.subtract, ALU.mult),
                      ev, *before)

        def send_rows(dst, sem, g, src_, ready):
            def send(e):
                r = base_reg(e, bai[0:1, g:g + 1], N - 128)
                return e.dma_start(dst[bass.ds(r, 128), :], src_)
            wrote[sem] = dma("sp", send, sem, ready, wrote[sem], base_done)
            return wrote[sem]

        xw_in = {}

        def load_xw(g):
            def send(e):
                r = base_reg(e, bai[0:1, g:g + 1], N - 128)
                return e.dma_start(xw[:, g % 2, :], x[bass.ds(r, 128), :])
            xw_in[g] = dma("sp", send, f"xw{g % 2}", base_done, *free(("xw", g % 2)))

        def first_post(g):
            s = g % 2

            def f():
                ev = op("dve", lambda e: e.tensor_tensor(hw[:, s, :], Pg[:, s, :], b1[:, :], ALU.add), pg_at[g], ldw, *free(("hw", s)))
                fr.setdefault(("pg", s), []).append(ev)
                ev = op("act", lambda e: e.activation(h1w[:, s, :], hw[:, s, :], ACT.Relu), ev, *free(("h1w", s)))
                fr["hw", s] = [ev]
                fr["h1w", s] = [send_rows(H1, "h1", g, h1w[:, s, :], ev)]
            return [f]

        def second_post(g):
            s = g % 2
            tb, ready = (bank[1], []) if g < NW - 1 else (bank[4], [("zt", 0)])
            box = {}

            def a():
                ev = op("dve", lambda e: e.tensor_tensor(hw[:, s, :], Pg[:, s, :], b2[:, :], ALU.add), pg_at[g], *free(("hw", s)))
                fr.setdefault(("pg", s), []).append(ev)
                ev = op("dve", lambda e: e.tensor_tensor(hw[:, s, :], hw[:, s, :], xw[:, s, :], ALU.add), ev, xw_in[g])
                fr["xw", s] = [ev]
                box["std"] = spread(hw[:, s, :], 128, s, ev)

            def a2():
                ev = scale(hw[:, s, :], h1w[:, s, :], 128, s, box["std"], *free(("h1w", s)))
                fr["hw", s] = [ev]
                box["x1"] = ev
                fr["h1w", s] = [send_rows(X1, "x1", g, h1w[:, s, :], ev)]
                if g + 2 < NW:
                    load_xw(g + 2)

            def b():
                Q.wait("pe", box["x1"], *free("tr"), *[x for k in ready for x in free(k)])
                for k in range(2):
                    ev = op("pe", lambda e, k=k: e.transpose(tb[:, k * 128:(k + 1) * 128], h1w[:, s, k * 128:(k + 1) * 128],
                                                             idn[:, :]), sig=(k == 1))
                fr["h1w", s].append(ev)
                ev = op("act", lambda e: e.copy(xT[:, s, :], tb[:, 0:256]), ev, *free(("xT", s)))
                fr["tr"] = [ev]

            def c():
                Q.wait("pe", fr["tr"][0])
                for mo in range(2):
                    for k in range(2):
                        ev = op("pe", lambda e, k=k, mo=mo: e.matmul(tb[:, 256 + 128 * mo:384 + 128 * mo],
                                                                     wts[:, 0, k, mo * 128:(mo + 1) * 128],
                                                                     xT[:, s, k * 128:(k + 1) * 128], start=(k == 0), stop=(k == 1)),
                                sig=(k == 1))
                fr["xT", s] = [ev]
                for mo in range(2):
                    def put(e, mo=mo):
                        r = base_reg(e, bai[0:1, g:g + 1], N - 128)
                        return e.activation(hT[:, mo, bass.ds(r, 128)], tb[:, 256 + 128 * mo:384 + 128 * mo], ACT.Identity,
                                            bias=bT[:, mo:mo + 1])
                    ev = op("act", put, ev, marks["codes"])
                fr["tr"] = [ev]
                marks["h0"] = ev
            return [a, a2, b, c]

        def apply(layer, g):
            W = (W1, W2)[layer]
            s = g % 2

            def part(n):
                def f():
                    if n == 0:
                        Q.wait("pe", z_at[layer, g], marks["W", layer], marks["W1pe"], *free("p"))
                    for q in range(2 * n, 2 * n + 2):
                        k, r = divmod(q, 8)
                        ev = op("pe", lambda e, q=q, k=k, r=r: e.matmul(bank[0][:, 0:256], ZA[:, s, q, 0:128],
                                                                        W[:, k, r * 256:(r + 1) * 256], start=(q == 0),
                                                                        stop=(g == 0 and q == 15)), sig=(q == 15))
                    if n == 7:
                        fr["za", s] = [ev]
                        fr["W1"] = [ev]
                        if g > 0:
                            ev = op("pe", lambda e: e.matmul(bank[0][:, 0:256], Ew[:, s, :], Pg[:, 1 - s, :], start=False, stop=True),
                                    marks["e1"], pg_at[g - 1])
                            fr["e1", s] = [ev]
                            fr.setdefault(("pg", 1 - s), []).append(ev)
                        ev = op("act", lambda e: e.copy(Pg[:, s, :], bank[0][:, 0:256]), ev, *free(("pg", s)))
                        fr["pg", s] = []
                        fr["p"] = [ev]
                        pg_at[g] = ev
                return f

            def sel():
                if g > 0:
                    marks["e1"] = op("dve", lambda e: e.tensor_scalar(Ew[:, s, :], iot[:, :], pd1[:, g:g + 1], None, ALU.is_equal),
                                     pd_done, *free(("e1", s)))
                part(0)()
            return [sel] + [part(n) for n in range(1, 8)]

        g_sl = [0]

        def clear(g, k):
            o = ZA[:, g % 2, 4 * k:4 * k + 4, :].rearrange("p q c -> p (q c)")
            marks["za", g] = op("act", lambda e: e.copy(o, zero[:, 0:1].to_broadcast([128, 4 * ZC])), zero_done,
                                *free(("za", g % 2)))

        def relational(layer, table, ready, extra):
            todo, sel_at, sel_n = {}, {}, [0]
            Q.wait("pool", *ready)
            for t in range(T):
                w, i = divmod(t, TA)
                g, wi = divmod(w, SW)
                n = g_sl[0]
                g_sl[0] += 1
                sl, ss, zb = n % NG, n % NSL, w % 2
                K = edge_rows(t)
                if t == 0:
                    for k in range(4):
                        clear(0, k)
                if t % TW in (24, 25, 26, 27) and g + 1 < NW:
                    clear(g + 1, t % TW - 24)
                ge = gathered[n] if n < FIRST else gather(n, t, table, *free(("g", sl)))
                while sel_n[0] < min(T, t + AHEAD):
                    u = sel_n[0]
                    sel_n[0] += 1
                    us = (n - t + u) % NSL
                    sel_at[u] = op("dve", lambda e, us=us, u=u: e.tensor_scalar(S[:, us, :], iot[:, :], c2[:, u:u + 1], wgt[:, u:u + 1],
                                                                                ALU.is_equal, ALU.mult), c2_done, *free(("s", us)))
                se = sel_at[t]
                ev = op("pe", lambda e, sl=sl, ss=ss, i=i, K=K, zb=zb: e.matmul(
                    bank[2 + zb][:, 0:256], S[0:K, ss, :], G[0:K, sl, :], start=(i == 0), stop=(i == TA - 1)),
                    ge, se, *(free(("z", zb)) if i == 0 else []))
                fr["g", sl] = fr["s", ss] = [ev]
                if i == TA - 1:
                    ev = op("act", lambda e, zb=zb: e.copy(Zs[:, zb, :], bank[2 + zb][:, 0:256]), ev, *free(("zs", zb)))
                    fr["z", zb] = [ev]

                    def turn(w=w, g=g, zb=zb, ev=ev, wi=wi):
                        Q.wait("pe", ev, idn_done, *free(("zt", zb)))
                        for k in range(2):
                            e2 = op("pe", lambda e, k=k: e.transpose(bank[4 + zb][:, k * 128:(k + 1) * 128],
                                                                     Zs[:, zb, k * 128:(k + 1) * 128], idn[:, :]), sig=(k == 1))
                        fr["zs", zb] = [e2]

                        def add(e):
                            r = base_reg(e, off[0:1, w:w + 1], 127)
                            o = ZA[:, g % 2, :, bass.ds(r, 16)]
                            return e.tensor_tensor(o, o, bank[4 + zb][:, 0:256].rearrange("p (q c) -> p q c", c=16), ALU.add)
                        z_at[layer, g] = op("dve", add, e2, marks["za", g] if wi == 0 else z_at[layer, g], off_done)
                        fr["zt", zb] = [z_at[layer, g]]
                    todo.setdefault(t + 2, []).append(turn)
                    if wi == SW - 1 or t == T - 1:
                        start, by = (41, 1) if layer == 0 and g == 0 else (t + 4, 2) if g < NW - 2 else (t + 3, 1)
                        post = first_post(g) if layer == 0 else second_post(g)
                        for k, f in enumerate(apply(layer, g) + [lambda: None] + post):
                            todo.setdefault(start + by * k, []).append(f)
                for f in todo.pop(t, []):
                    f()
                extra(layer, t)
            return [f for t in sorted(todo) for f in todo[t]]

        state = {"a": 0, "load": 0, "deg": 0}
        dsum = {}

        def degree_sum():
            c = state["deg"]
            if c < N // DG:
                state["deg"] += 1
                a = A_sb[0:PB, :, c * DG:(c + 1) * DG].rearrange("p j n -> p n j")
                dsum[c * DG // CH] = op("dve", lambda e: e.tensor_reduce(rdeg[0:PB, c * DG:(c + 1) * DG], a, AX, ALU.add), marks["A"])

        def extra(layer, t):
            n = layer * T + t
            if layer == 0:
                for _ in range(min(len(chores), 1 + (t % 3 == 0) if t < 40 else 1 - t % 2)):
                    chores.pop(0)()
                if products:
                    products.pop(0)()
                if t == 88:
                    fr["qa", 0], fr["qa", 1] = [marks["wb", 0]], [marks["wb", 1]]
            while state["a"] < T and n >= 90 + state["a"] * 1.65 and not T - 10 <= n < T:
                adjacency_tile(state["a"])
                state["a"] += 1
            if n > 1158 and n % 3 == 0 and state["load"] < JB:
                j = state["load"]
                state["load"] += 1
                marks["A"] = dma("act", lambda e: e.dma_start(A_sb[0:PB, j, :], Ad[j * PB:(j + 1) * PB, 0:N]), "ar",
                                 wrote["aw"], marks["W", 1], *free("W1"))

            if 1230 < n < 2 * T - 14 and n % 4 == 0:
                degree_sum()

        for f in relational(0, x, [], extra):
            f()
        assert not chores
        while state["a"] < 350:
            adjacency_tile(state["a"])
            state["a"] += 1
        fr["xw", 0] = fr["xw", 1] = list(diag_free)
        load_xw(0)
        load_xw(1)
        rest = relational(1, H1, [wrote["h1"]], extra)
        assert state["a"] == T and state["load"] == JB

        def queued():
            return [(k, Q.n[k]) for k in ("pe", "act", "dve")] + [wrote["aw"]]

        assert AHEAD_HS * 512 + NR * CH <= 8512
        last = 13
        for f in rest[:-last]:
            f()
        over = {"a": queued()}
        bf = {0: None, 1: marks["h0"], 2: fr["z", 0][0], 3: fr["z", 1][0], 5: fr["zt", 1][0], 6: fr["qa", 0][0], 7: fr["qa", 1][0]}

        def bfree(b):
            return [bf[b]]

        hs_read = [None]
        hs_at = [None] * JB
        h_at = [marks["h0"]] * (NC - 1) + [None]
        rd = [None] * NC
        ar_read = [None] * NR
        cnt = {"nm": 0, "ar": 0}

        def node_major(j):
            b = (6, 7, 2, 3)[cnt["nm"] % 4]
            cnt["nm"] += 1
            Q.wait("pe", h_at[j // 4], *bfree(b))
            for k in range(2):
                ev = op("pe", lambda e, k=k: e.transpose(bank[b][0:PB, k * 128:(k + 1) * 128], hT[:, k, j * PB:(j + 1) * PB],
                                                         idn[:, :]), sig=(k == 1))
            ov = over["a" if j < AHEAD_HS else "b"]
            ev = op("act", lambda e: e.copy(hs[0:PB, j, 0, :], bank[b][0:PB, 0:256]), ev, hs_read[0], *ov)
            ev = op("dve", lambda e: e.tensor_tensor(hs[0:PB, j, 1, :], bank[b][0:PB, 0:256], hs[0:PB, j, 0, :].bitcast(F32),
                                                     ALU.subtract), ev, hs_read[0], *ov)
            bf[b] = ev
            hs_at[j] = ev

        ar_at = {}

        def convert(n):
            l, q = divmod(n, NC * JB)
            c, j = divmod(q, JB)
            sl = n % NR
            i_ = A_sb[0:PB, j, c * CH:(c + 1) * CH]
            o = Ar[0:PB, sl, :]
            if l == 0 or n % 2:
                ar_at[n] = op("act", lambda e: e.copy(o, i_), ar_read[sl], marks["A"], *over["a"])
            else:
                ar_at[n] = op("dve", lambda e: e.tensor_copy(o, i_), ar_read[sl], marks["A"], *over["a"])

        def degree(c):
            rc = rdeg[:, c * CH:(c + 1) * CH]
            ev = op("pe", lambda e: e.matmul(bank[5][:, 0:CH], onef[0:PB, :], rc[0:PB, :], start=True, stop=True), dsum[c], *bfree(5))
            ev = op("dve", lambda e: e.tensor_scalar(rc, bank[5][:, 0:CH], 1.0, None, ALU.max), ev)
            bf[5] = ev
            rd[c] = op("dve", lambda e: e.reciprocal(rc, rc), ev)

        def aggregate(l, c, beside):
            s = c % 2
            bs = [2 * s, 2 * s + 1]
            for b in bs:
                Q.wait("pe", *bfree(b))
            for j in range(JB):
                n = (l * NC + c) * JB + j
                while cnt["ar"] < min(3 * NC * JB, n + 7):
                    convert(cnt["ar"])
                    cnt["ar"] += 1
                beside(j)
                Q.wait("pe", ar_at[n], hs_at[j])
                o = Ar[0:PB, n % NR, :]
                for mo in range(2):
                    for q in range(2):
                        ev = op("pe", lambda e, mo=mo, q=q, j=j, o=o: e.matmul(
                            bank[bs[mo]][:, 0:CH], hs[0:PB, j, q, mo * 128:(mo + 1) * 128], o,
                            start=(j == 0 and q == 0), stop=(j == JB - 1 and q == 1)), sig=(mo == 1 and q == 1))
                ar_read[n % NR] = ev
            hs_read[0] = ev
            rc = rdeg[:, c * CH:(c + 1) * CH]
            for mo in range(2):
                ev = op("dve", lambda e, mo=mo: e.tensor_tensor(agT[:, s, mo, :], bank[bs[mo]][:, 0:CH], rc, ALU.mult),
                        ev if mo == 0 else None, rd[c], fr.get(("ag", s)), *over["b"])
                bf[bs[mo]] = ev
            while cnt["ar"] < min(3 * NC * JB, n + 8):
                convert(cnt["ar"])
                cnt["ar"] += 1
            return ev

        def combine(l, c, ready):
            s = c % 2
            for q in range(4):
                k2, mo = divmod(q, 2)
                b = 4 + mo
                if q < 2:
                    Q.wait("pe", *bfree(b), h_at[c])
                if q == 2:
                    Q.wait("pe", ready)
                for k in range(2):
                    w_ = wts[:, 2 + 2 * l - k2, k, mo * 128:(mo + 1) * 128]
                    r_ = agT[:, s, k, :] if k2 else hT[:, k, c * CH:(c + 1) * CH]
                    ev = op("pe", lambda e, b=b, w_=w_, r_=r_, k=k, k2=k2: e.matmul(bank[b][:, 0:CH], w_, r_, start=(k + k2 == 0),
                                                                                    stop=(k + k2 == 2)), sig=(k + k2 == 2))
            fr["ag", s] = ev
            for mo in range(2):
                b = 4 + mo
                ev2 = op("act", lambda e, b=b, mo=mo: e.activation(hT[:, mo, c * CH:(c + 1) * CH], bank[b][:, 0:CH], ACT.Relu,
                                                                   bias=bT[:, 2 + 2 * l + mo:3 + 2 * l + mo]), ev)
                bf[b] = ev2
            h_at[c] = ev2

        lx = {}
        xr = [None] * 4
        o_free = [None] * 4

        def load_x1(j):
            lx[j] = dma("sp", lambda e: e.dma_start(x1b[0:PB, j % 4, :], X1[j * PB:(j + 1) * PB, :]), f"xs{j % 4}", xr[j % 4], wrote["x1"], *over["c"])

        def add_bias(j):
            x_ = x1b[0:PB, j % 4, :]
            lx[j] = op("dve", lambda e: e.tensor_tensor(x_, x_, bo[0:PB, :], ALU.add), lx[j])

        def output(j):
            s = j % 4
            b = (6, 7, 2, 3)[j % 4] if j >= JB - 4 else 6 + j % 2
            Q.wait("pe", h_at[j // 4], *bfree(b))
            for k in range(2):
                ev = op("pe", lambda e, k=k: e.matmul(bank[b][0:PB, 0:256], hT[:, k, j * PB:(j + 1) * PB], wts[:, 7, k, :],
                                                      start=(k == 0), stop=(k == 1)), sig=(k == 1))
            y, o = yb[0:PB, s, :], ob[0:PB, s, :]
            ev = op("dve", lambda e: e.tensor_tensor(y, bank[b][0:PB, 0:256], x1b[0:PB, s, :], ALU.add), ev, lx[j])
            bf[b] = xr[s] = ev
            if j + 4 < JB:
                load_x1(j + 4)
            std[j] = spread(y, PB, s, ev)
            if j + 2 < JB:
                add_bias(j + 2)

        std = {}

        def output_end(j):
            s = j % 4
            y, o = yb[0:PB, s, :], ob[0:PB, s, :]
            ev = scale(y, o, PB, s, std[j], o_free[s])
            o_free[s] = dma("sp", lambda e: e.dma_start(out[j * PB:(j + 1) * PB, :], o), f"o{s}", ev)

        while cnt["ar"] < NR:
            convert(cnt["ar"])
            cnt["ar"] += 1
        for f in rest[-last:-4]:
            f()
        bf[0] = pg_at[NW - 1]
        for j in range(4):
            node_major(j)
        rest[-4]()
        for j in range(4, AHEAD_HS):
            node_major(j)
        rest[-3]()
        over["b"] = queued()
        early = AHEAD_HS
        for l in range(3):
            made = [early]
            if l == 2:
                for j in range(4):
                    load_x1(j)
            ag = {}
            for c in range(NC):
                def beside(j, l=l, c=c):
                    if c == 0:
                        while made[0] < min(JB, j + 4):
                            node_major(made[0])
                            made[0] += 1
                    if l == 0 and c == 0 and j in (2, 4):
                        rest[-2 if j == 2 else -1]()
                        h_at[NC - 1] = bf[4] = marks["h0"]
                        over["c"] = queued()
                    if l == 0 and j % 3 == 1 and (c > 0 or j > 8):
                        degree_sum()
                    if l == 0 and j == 17:
                        degree(c)
                    if c > 0 and j == 5:
                        combine(l, c - 1, ag[c - 1])
                    if l == 2 and c == 1 and j == 3:
                        add_bias(0)
                        add_bias(1)
                    if l == 2 and c > 0 and j > 7:
                        i = j - 8
                        if i % 3 == 0 and i < 12:
                            output(4 * (c - 1) + i // 3)
                        if i % 3 == 2:
                            output_end(4 * (c - 1) + i // 3)
                ag[c] = aggregate(l, c, beside)
            if l < 2:
                for j in range(4):
                    node_major(j)
            combine(l, NC - 1, ag[NC - 1])
            if l < 2:
                for j in range(4, 8):
                    node_major(j)
            early = 8
        for j in range(JB - 4, JB):
            output(j)
            if j > JB - 4:
                output_end(j - 1)
        output_end(JB - 1)
        Q.wait("sp", *o_free)

        block = ctx.enter_context(nc.Block())

        def run(eng, e):
            for f in Q.ops[eng][:head[eng]]:
                f(e)
            e.wait_ge(sems["dve"], flag_done[1])
            fast = e.value_load(flag[0:1, 0:1], min_val=0, max_val=1)
            with e.If(fast):
                for f in Q.ops[eng][head[eng]:]:
                    f(e)
            with e.Else():
                if eng == "dve":
                    for name, n in all_done:
                        if n:
                            e.wait_ge(sems[name], n)
                    e.sem_inc(sems["k_" + relay.first(relay.top[0])], 1)
                relay.emit(eng, e, relay.top, None, {})

        @block.tensor
        def _(e):
            run("pe", e)

        @block.scalar
        def _(e):
            run("act", e)

        @block.vector
        def _(e):
            run("dve", e)

        @block.gpsimd
        def _(e):
            run("pool", e)

        @block.sync
        def _(e):
            run("sp", e)


def kernel(x, src, dst, edge_type_8, edge_weight1, L0_gnn_basis, L0_gnn_coeff, L0_gnn_bias, L1_gnn_W_in, L1_gnn_b_in,
           L1_gnn_W_agg, L1_gnn_W_self, L1_gnn_b_hid, L1_gnn_W_out, L1_gnn_b_out):
    import numpy as np
    import concourse.bacc as bacc
    from concourse import mybir as mb
    from concourse.bass_utils import run_bass_kernel_spmd as run

    def tiles(a, pad):
        a = np.asarray(a).reshape(-1)
        a = np.concatenate([a, np.full(T * 128 - E, pad, a.dtype)])
        return np.ascontiguousarray(a.reshape(T, 128).T)

    dst = np.asarray(dst)
    arrays = {
        "x": np.asarray(x),
        "srcT": tiles(src, 0),
        "dstT": tiles(dst, N - 1),
        "etT": tiles(edge_type_8, 0),
        "wT": tiles(edge_weight1, 0.0),
        "large": np.ascontiguousarray(dst[::TW * 128].reshape(1, NW)),
        "small": np.ascontiguousarray(dst[::TA * 128].reshape(1, NA)),
        "basis": np.asarray(L0_gnn_basis),
        "coeff": np.asarray(L0_gnn_coeff).reshape(1, 128),
        "bias": np.asarray(L0_gnn_bias),
        "W_in": np.asarray(L1_gnn_W_in),
        "b_cols": np.ascontiguousarray(np.concatenate([np.asarray(L1_gnn_b_in).reshape(2, 128),
                                                       np.asarray(L1_gnn_b_hid).reshape(6, 128)]).T),
        "b_rows": np.concatenate([np.asarray(L1_gnn_b_in).reshape(1, D), np.asarray(L1_gnn_b_hid)]).reshape(1, 4 * D),
        "W_agg": np.asarray(L1_gnn_W_agg),
        "W_self": np.asarray(L1_gnn_W_self),
        "W_out": np.asarray(L1_gnn_W_out),
        "b_out": np.asarray(L1_gnn_b_out).reshape(1, D),
    }
    arrays = {k: np.ascontiguousarray(v) for k, v in arrays.items()}
    nc = bacc.Bacc("TRN2", target_bir_lowering=False, num_devices=1)
    h = {k: nc.dram_tensor("in_" + k, v.shape, mb.dt.from_np(v.dtype), kind="ExternalInput").ap() for k, v in arrays.items()}
    o = nc.dram_tensor("out", (N, D), mb.dt.float32, kind="ExternalOutput").ap()
    program(nc, h["x"], h["srcT"], h["dstT"], h["etT"], h["wT"], h["large"], h["small"], h["basis"], h["coeff"], h["bias"],
            h["W_in"], h["b_cols"], h["W_agg"], h["W_self"], h["b_rows"], h["W_out"], h["b_out"], o)
    r = run(nc, [{"in_" + k: v for k, v in arrays.items()}], core_ids=[0])
    return r.results[0]["out"]
```
